# Optimizing a Trainium2 kernel written in Bass

```python
import numpy as np
import jax
import jax.numpy as jnp

def _softmax(x, axis=-1):
    return jax.nn.softmax(x, axis=axis)

def _gelu(x):
    return jax.nn.gelu(x, approximate=True)

def _silu(x):
    return jax.nn.silu(x)

def _sigmoid(x):
    return jax.nn.sigmoid(x)

def _layernorm(x, axis=-1, eps=1e-05):
    m = jnp.mean(x, axis=axis, keepdims=True)
    v = jnp.var(x, axis=axis, keepdims=True)
    return (x - m) / jnp.sqrt(v + eps)

def _scatter_add(tgt, idx, src, axis=0):
    return tgt.at[idx].add(src)

def _segment_sum(src, seg, n):
    return jax.ops.segment_sum(src, seg, n)
kernel_name = 'mk_gnn_preln_d1_gnn_r32_5bd920'

def setup_inputs(seed: int=0):
    np.random.seed(seed)
    _w = jnp.asarray

    def _rec_inputs():
        import jax
        import jax.numpy as jnp
        _gk = jax.random.key(seed)
        x = -0.0005121 + 1.001 * jax.random.normal(jax.random.fold_in(_gk, 1), (3125, 64), jnp.float32)
        _s = jax.random.randint(jax.random.fold_in(_gk, 2), (25000,), 0, 3125, jnp.int32)
        _d = jax.random.randint(jax.random.fold_in(_gk, 3), (25000,), 0, 3125, jnp.int32)
        _loop = jnp.arange(3125, dtype=jnp.int32)
        src = jnp.concatenate([_s, _d, _loop])
        dst = jnp.concatenate([_d, _s, _loop])
        _o = jnp.argsort(dst, stable=True)
        src = src[_o]
        dst = dst[_o]
        edge_attr_3 = 0.000669165 + 0.999965 * jax.random.normal(jax.random.fold_in(_gk, 11), (53125, 3), jnp.float32)
        return (x, src, dst, edge_attr_3)
    x, src, dst, edge_attr_3 = _rec_inputs()

    def _L0_gnn_setup():
        import jax, jax.numpy as jnp
        import numpy as np
        N_NODES = 50000
        N_EDGES = 25000
        IN_NF = 64
        HID_NF = 64
        OUT_NF = 64

        def _linear_init(key, fan_in, fan_out):
            kw, kb = jax.random.split(key)
            bound = 1.0 / np.sqrt(fan_in)
            W = jax.random.uniform(kw, (fan_in, fan_out), jnp.float32, -bound, bound)
            b = jax.random.uniform(kb, (fan_out,), jnp.float32, -bound, bound)
            return (W, b)
        key = jax.random.key(seed)
        ks = jax.random.split(key, 9)
        h = jax.random.normal(ks[0], (N_NODES, IN_NF), jnp.float32)
        edges_index = jax.random.randint(ks[1], (2, N_EDGES), 0, N_NODES, jnp.int64)
        coord_diff = jax.random.normal(ks[2], (N_EDGES, 3), jnp.float32)
        We1, be1 = _linear_init(ks[3], 2 * IN_NF + 1, HID_NF)
        We2, be2 = _linear_init(ks[4], HID_NF, HID_NF)
        Wa, ba = _linear_init(ks[5], HID_NF, 1)
        Wn1, bn1 = _linear_init(ks[6], HID_NF + IN_NF, HID_NF)
        Wn2, bn2 = _linear_init(ks[7], HID_NF, OUT_NF)
        return {'h': h, 'edges_index': edges_index, 'coord_diff': coord_diff, 'We1': We1, 'be1': be1, 'We2': We2, 'be2': be2, 'Wa': Wa, 'ba': ba, 'Wn1': Wn1, 'bn1': bn1, 'Wn2': Wn2, 'bn2': bn2}
    _L0_gnn_all = _L0_gnn_setup()
    _L0_gnn_in = {k: v for k, v in _L0_gnn_all.items() if k in ('We1', 'be1', 'We2', 'be2', 'Wa', 'ba', 'Wn1', 'bn1', 'Wn2', 'bn2')}
    del _L0_gnn_all
    return {'x': x, 'src': src, 'dst': dst, 'edge_attr_3': edge_attr_3, 'L0_gnn_We1': _L0_gnn_in['We1'], 'L0_gnn_be1': _L0_gnn_in['be1'], 'L0_gnn_We2': _L0_gnn_in['We2'], 'L0_gnn_be2': _L0_gnn_in['be2'], 'L0_gnn_Wa': _L0_gnn_in['Wa'], 'L0_gnn_ba': _L0_gnn_in['ba'], 'L0_gnn_Wn1': _L0_gnn_in['Wn1'], 'L0_gnn_bn1': _L0_gnn_in['bn1'], 'L0_gnn_Wn2': _L0_gnn_in['Wn2'], 'L0_gnn_bn2': _L0_gnn_in['bn2']}

def reference(x, src, dst, edge_attr_3, L0_gnn_We1, L0_gnn_be1, L0_gnn_We2, L0_gnn_be2, L0_gnn_Wa, L0_gnn_ba, L0_gnn_Wn1, L0_gnn_bn1, L0_gnn_Wn2, L0_gnn_bn2):
    import jax
    import jax.numpy as jnp

    def _L0_gnn_ref(h, edges_index, coord_diff, We1, be1, We2, be2, Wa, ba, Wn1, bn1, Wn2, bn2):
        import jax, jax.numpy as jnp
        import numpy as np
        N_NODES = 50000
        N_EDGES = 25000
        IN_NF = 64
        HID_NF = 64
        OUT_NF = 64

        def _linear_init(key, fan_in, fan_out):
            kw, kb = jax.random.split(key)
            bound = 1.0 / np.sqrt(fan_in)
            W = jax.random.uniform(kw, (fan_in, fan_out), jnp.float32, -bound, bound)
            b = jax.random.uniform(kb, (fan_out,), jnp.float32, -bound, bound)
            return (W, b)
        row = edges_index[0]
        col = edges_index[1]
        radial = jnp.sum(coord_diff ** 2, axis=1, keepdims=True)
        edge_in = jnp.concatenate([h[row], h[col], radial], axis=1)
        e = jax.nn.silu(edge_in @ We1 + be1)
        e = jax.nn.silu(e @ We2 + be2)
        att = jax.nn.sigmoid(e @ Wa + ba)
        e = e * att
        agg = jax.ops.segment_sum(e, row, num_segments=h.shape[0])
        node_in = jnp.concatenate([h, agg], axis=1)
        out = jax.nn.silu(node_in @ Wn1 + bn1) @ Wn2 + bn2
        return out
    edge_index = jnp.stack([src, dst])
    h = jnp.maximum(_layernorm(x, axis=-1), 0.0)
    x = x + _L0_gnn_ref(h, edge_index, edge_attr_3, L0_gnn_We1, L0_gnn_be1, L0_gnn_We2, L0_gnn_be2, L0_gnn_Wa, L0_gnn_ba, L0_gnn_Wn1, L0_gnn_bn1, L0_gnn_Wn2, L0_gnn_bn2)
    return x

_drawn_inputs = setup_inputs


def setup_inputs(seed=0):
    import zlib

    import numpy as np

    out = dict(_drawn_inputs(seed))
    spreads = {}
    factors = {'edge_attr_3': 200.0,
     'L0_gnn_be1': 200.0,
     'L0_gnn_Wa': 8.0,
     'L0_gnn_bn1': 3.535,
     'L0_gnn_be2': 47.144,
     'L0_gnn_We1': 8.0}
    for name, (base, spread) in spreads.items():
        noise = np.random.default_rng([zlib.crc32(name.encode()), seed]).standard_normal(out[name].shape)
        drawn = base * np.exp(spread * noise) if base else spread * noise
        out[name] = jnp.asarray(drawn.astype(out[name].dtype))
    for name, factor in factors.items():
        out[name] = (out[name] * factor).astype(out[name].dtype)
    return out
```

```python
import concourse.bass as bass
from concourse import mybir
from contextlib import ExitStack


def graph_layer(nc, x, src, dst, edge_attr, We1, be1, We2, be2, Wa, ba, Wn1, bn1, Wn2, bn2, out):
    f32 = mybir.dt.float32
    i32 = mybir.dt.int32
    u32 = mybir.dt.uint32
    i16 = mybir.dt.int16
    ALU = mybir.AluOpType
    ACT = mybir.ActivationFunctionType
    AX = mybir.AxisListType

    NODES, F = x.shape
    EDGES = src.shape[0]
    P = 128
    TILES = 4
    CH = TILES * P
    CHUNKS = -(-EDGES // CH)
    FULL = EDGES // CH
    REST = EDGES - FULL * CH
    SLOTS = 8
    ROUNDS = CHUNKS // SLOTS
    LEAD = 6
    WIN = 112
    NP = 125
    NB = NODES // NP
    SPARE = 3136
    ROWS = SPARE + P
    ACCS = 2
    PER_ACC = TILES // ACCS
    EPS = 1e-5
    GROUP = 4
    GROUPS = [range(g, min(g + GROUP, NB)) for g in range(0, NB, GROUP)]
    SPLIT = 96
    assert NP * NB == NODES and ROUNDS * SLOTS == CHUNKS and CHUNKS <= P and FULL == CHUNKS - 1
    assert NODES + WIN <= ROWS and NODES < SPARE and (ROWS * F) % P == 0

    ctx = ExitStack()
    with ctx:
        def sb(name, shape, dt=f32):
            return ctx.enter_context(nc.sbuf_tensor(name, shape, dt))

        def pb(name, shape):
            return ctx.enter_context(nc.psum_tensor(name, shape, f32))

        def sem(name):
            return ctx.enter_context(nc.semaphore(name))

        def dram(name, shape, dt=f32):
            return nc.dram_tensor(name, shape, dt, kind="Internal").ap()

        a_table = dram("a_table", [ROWS, F])
        b_table = dram("b_table", [ROWS, F])
        acc = [dram(f"acc{k}", [ROWS, F]) for k in range(ACCS)]
        src_rows = dram("src_rows", [CHUNKS, CH], i16)
        dst_rows = dram("dst_rows", [CHUNKS, CH], i16)
        radial_rows = dram("radial_rows", [CHUNKS, CH])

        ident = sb("ident", [P, P])
        ones = sb("ones", [P, P])
        earlier = sb("earlier", [P, P])
        channel = sb("channel", [P, 1])
        zeros = sb("zeros", [P, ROWS * F // P])
        we1ab = sb("we1ab", [F, 2 * F])
        we2 = sb("we2", [F + 1, F])
        wn1 = sb("wn1", [F, 2, F])
        wn2 = sb("wn2", [F + 1, F])
        wa = sb("wa", [P, F])
        ba_col = sb("ba_col", [P, 1])
        be1_col = sb("be1_col", [F, 1])
        bn1_col = sb("bn1_col", [F, 1])

        xs = sb("xs", [NP, NB, F])
        xc = sb("xc", [NP, NB, F])
        h = sb("h", [NP, NB, F])
        stat = sb("stat", [NP, 6, NB])
        hT = sb("hT", [F, NB * NP])
        a_out = sb("a_out", [NP, NB, F])
        b_out = sb("b_out", [NP, NB, F])

        src_i = sb("src_i", [CHUNKS, CH], i32)
        dst_i = sb("dst_i", [CHUNKS, CH], i32)
        src_f = sb("src_f", [CHUNKS, CH])
        dst_f = sb("dst_f", [CHUNKS, CH])
        src_h = sb("src_h", [CHUNKS, CH], i16)
        dst_h = sb("dst_h", [CHUNKS, CH], i16)
        attr = sb("attr", [CHUNKS, CH, 3])
        attr2 = sb("attr2", [CHUNKS, CH, 3])
        radial = sb("radial", [CHUNKS, CH])
        spread = sb("spread", [CHUNKS, 1])
        diag = sb("diag", [CHUNKS, 2, CHUNKS])
        src_cols = sb("src_cols", [P, CHUNKS, TILES])
        dst_cols = sb("dst_cols", [P, CHUNKS, TILES])
        to_spare = sb("to_spare", [P, CHUNKS, TILES])
        worst = sb("worst", [P, 1])
        fits = sb("fits", [P, 1])
        fits_i = sb("fits_i", [1, 1], i32)
        win_row = sb("win_row", [P, CHUNKS])

        src_bc = [sb(f"src_bc{s}", [P, CH], i16) for s in range(SLOTS)]
        dst_bc = [sb(f"dst_bc{s}", [WIN, CH], i16) for s in range(SLOTS)]
        window = [sb(f"window{s}", [WIN + 1, F]) for s in range(SLOTS)]
        onehot = [sb(f"onehot{s}", [WIN + 1, CH]) for s in range(SLOTS)]
        gath = [sb(f"gath{s}", [P, TILES * F]) for s in range(SLOTS)]
        gidx_a = [[sb(f"gidx{s}_{j}", [P, 1], u32) for j in range(TILES)] for s in range(SLOTS)]
        gidx_b = [[sb(f"gidxb{s}_{j}", [P, 1], u32) for j in range(TILES)] for s in range(SLOTS)]
        sidx = [[sb(f"sidx{s}_{j}", [P, 1], u32) for j in range(TILES)] for s in range(SLOTS)]
        summed = [sb(f"summed{s}", [P, TILES * F]) for s in range(SLOTS)]
        sig1 = [sb(f"sig1_{d}", [F, CH]) for d in range(2)]
        e1 = [sb(f"e1_{d}", [F + 1, CH]) for d in range(2)]
        sig2 = [sb(f"sig2_{d}", [P, TILES, F]) for d in range(2)]
        e2 = [sb(f"e2_{d}", [P, TILES, F]) for d in range(2)]
        ewa = [sb(f"ewa{d}", [P, TILES, F]) for d in range(2)]
        logit = [sb(f"logit{d}", [P, TILES]) for d in range(2)]
        att = [sb(f"att{d}", [P, TILES]) for d in range(2)]
        same = [sb(f"same{d}", [P, TILES, P]) for d in range(2)]
        same_before = [sb(f"same_before{d}", [P, TILES, P]) for d in range(2)]
        dup = sb("dup", [P, TILES])
        shift = sb("shift", [P, TILES])

        aggs = [a_out, b_out]
        aggT = sb("aggT", [F, NB * NP])
        sig3 = sb("sig3", [F, NB * NP])
        n1 = sb("n1", [F + 1, NB * NP])
        result = xc

        z1 = [pb(f"z1_{d}", [P, 512]) for d in range(2)]
        z2 = [pb(f"z2_{d}", [P, 512]) for d in range(2)]
        zs = [pb(f"zs_{d}", [P, 512]) for d in range(2)]
        zt = [pb(f"zt_{d}", [P, 512]) for d in range(2)]
        BANKS = [*z1, *z2, *zs, *zt]

        padded = sem("padded")
        edges_in = sem("edges_in")
        attr_in = sem("attr_in")
        weights_in = sem("weights_in")
        x_in = sem("x_in")
        consts = sem("consts")
        dve_seq = sem("dve_seq")
        rows_made = sem("rows_made")
        rows_out = sem("rows_out")
        cols_in_psum = sem("cols_in_psum")
        cols_taken = sem("cols_taken")
        diag_made = sem("diag_made")
        spread_in_psum = sem("spread_in_psum")
        windows_known = sem("windows_known")
        var_made = sem("var_made")
        std_made = sem("std_made")
        h_made = sem("h_made")
        hT_in_psum = sem("hT_in_psum")
        hT_taken = sem("hT_taken")
        ab_in_psum = sem("ab_in_psum")
        ab_taken = sem("ab_taken")
        table_pads = sem("table_pads")
        tables_out = sem("tables_out")
        zeroed = sem("zeroed")
        src_in = [sem(f"src_in{s}") for s in range(SLOTS)]
        dst_in = [sem(f"dst_in{s}") for s in range(SLOTS)]
        win_in = [sem(f"win_in{s}") for s in range(SLOTS)]
        a_in = [sem(f"a_in{s}") for s in range(SLOTS)]
        b_in = [sem(f"b_in{s}") for s in range(SLOTS)]
        gidx_made = sem("gidx_made")
        pool_waits = sem("pool_waits")
        onehot_made = sem("onehot_made")
        z1_made = sem("z1_made")
        sig1_made = sem("sig1_made")
        e1_made = sem("e1_made")
        z2_made = sem("z2_made")
        sig2_made = sem("sig2_made")
        e2_made = sem("e2_made")
        ewa_made = sem("ewa_made")
        logit_made = sem("logit_made")
        att_made = sem("att_made")
        dup_made = sem("dup_made")
        shift_made = sem("shift_made")
        sidx_made = sem("sidx_made")
        same_made = sem("same_made")
        sum_made = sem("sum_made")
        sum_copied = sem("sum_copied")
        scattered = [sem(f"scattered{k}") for k in range(ACCS)]
        aggs_in = sem("aggs_in")
        agg_made = sem("agg_made")
        aggT_in_psum = sem("aggT_in_psum")
        aggT_taken = sem("aggT_taken")
        z3_made = sem("z3_made")
        sig3_made = sem("sig3_made")
        n1_made = sem("n1_made")
        y_made = sem("y_made")
        result_made = sem("result_made")
        result_out = sem("result_out")

        def after_scatters(c):
            return 16 * PER_ACC * c

        LOADED_W = 16 * (11 + SLOTS)

        def chunk_rounds(engine, step):
            for s in range(SLOTS):
                step(0, s, s, SLOTS)
            with engine.Fori(1, ROUNDS - 1) as n:
                for s in range(SLOTS):
                    step(n, s, SLOTS, SLOTS)
            for s in range(SLOTS):
                step(ROUNDS - 1, s, SLOTS, SLOTS - 1 - s)

        def previous(n, s):
            return (n, s - 1) if s else (n - 1, SLOTS - 1)

        block = ctx.enter_context(nc.Block())

        @block.sync
        def _(sp):
            sp.wait_ge(padded, 3)
            for flat, tile, done in ((dst, dst_i, edges_in), (src, src_i, edges_in)):
                v = flat[0:FULL * CH].rearrange("(c e) -> c e", e=CH)
                sp.dma_start(tile[0:SPLIT, :], v[0:SPLIT, :]).then_inc(done, 16)
                sp.dma_start(tile[SPLIT:FULL, :], v[SPLIT:FULL, :]).then_inc(done, 16)
                sp.dma_start(tile[FULL:CHUNKS, 0:REST], flat[FULL * CH:EDGES].rearrange("(c e) -> c e", c=1)).then_inc(done, 16)
            v = edge_attr[0:FULL * CH, :].rearrange("(c e) k -> c e k", e=CH)
            sp.dma_start(attr[0:SPLIT, :, :], v[0:SPLIT, :, :]).then_inc(attr_in, 16)
            sp.dma_start(attr[SPLIT:FULL, :, :], v[SPLIT:FULL, :, :]).then_inc(attr_in, 16)
            sp.dma_start(attr[FULL:CHUNKS, 0:REST, :],
                         edge_attr[FULL * CH:EDGES, :].rearrange("(c e) k -> c e k", c=1)).then_inc(attr_in, 16)
            sp.wait_ge(consts, 1)
            for table in (a_table, b_table):
                sp.dma_start(table[NODES:ROWS, :].rearrange("r f -> (r f)").rearrange("(p q) -> p q", p=F),
                             zeros[0:F, 0:ROWS - NODES]).then_inc(table_pads, 16)
            sp.wait_ge(rows_made, 1)
            sp.dma_start(dst_rows[:, :], dst_h[:, :]).then_inc(rows_out, 16)
            sp.wait_ge(rows_made, 2)
            sp.dma_start(src_rows[:, :], src_h[:, :]).then_inc(rows_out, 16)
            sp.wait_ge(rows_made, 3)
            sp.dma_start(radial_rows[:, :], radial[:, :]).then_inc(rows_out, 16)
            sp.wait_ge(rows_out, 48)

            def load_rows(c, s):
                sp.dma_start(dst_bc[s][:, :], bcast(dst_rows, c, WIN)).then_inc(dst_in[s], 16)
                sp.dma_start(src_bc[s][:, :], bcast(src_rows, c, P)).then_inc(src_in[s], 16)
                sp.dma_start(onehot[s][WIN:WIN + 1, :], radial_rows[bass.ds(c, 1), :]).then_inc(win_in[s], 16)

            def bcast(rows, c, n):
                return rows[bass.ds(c, 1), :].to_broadcast([n, CH])

            def load_window(c, s):
                first = sp.value_load(dst[bass.ds(c * CH, 1)].rearrange("(a b) -> a b", a=1),
                                      min_val=0, max_val=NODES - 1)
                sp.dma_start(window[s][0:WIN, :], b_table[bass.ds(first, WIN), :]).then_inc(win_in[s], 16)

            for s in range(SLOTS):
                load_rows(s, s)
            sp.wait_ge(table_pads, 32)
            sp.wait_ge(tables_out, 32)
            for s in range(SLOTS):
                load_window(s, s)

            def step(n, s):
                c = n * SLOTS + s
                sp.wait_ge(z1_made, c + 1)
                sp.wait_ge(same_made, c + 1)
                load_rows(c + SLOTS, s)
                load_window(c + SLOTS, s)

            with sp.Fori(0, ROUNDS - 1) as n:
                for s in range(SLOTS):
                    step(n, s)

            for k in range(ACCS):
                sp.wait_ge(scattered[k], after_scatters(CHUNKS))
                sp.dma_start(aggs[k][:, :, :],
                             acc[k][0:NODES, :].rearrange("(p b) f -> p b f", b=NB)).then_inc(aggs_in, 16)
            sp.wait_ge(result_made, len(GROUPS))
            sp.dma_start(out.rearrange("(p b) f -> p b f", b=NB), result[:, :, :]).then_inc(result_out, 16)
            sp.wait_ge(result_out, 16)

        @block.gpsimd
        def _(pool):
            nc.gpsimd.memset(ones[:, :], 1.0).then_inc(padded, 1)
            nc.gpsimd.memset(zeros[:, :], 0.0).then_inc(consts, 1)
            pool.wait_ge(padded, 3)
            nc.gpsimd.affine_select(out=ident[:, :], in_=ones[:, :], compare_op=ALU.is_equal, fill=0.0,
                                    base=0, pattern=[[-1, P]], channel_multiplier=1).then_inc(consts, 1)
            nc.gpsimd.affine_select(out=earlier[:, :], in_=ones[:, :], compare_op=ALU.is_gt, fill=0.0,
                                    base=0, pattern=[[-1, P]], channel_multiplier=1).then_inc(consts, 1)
            nc.gpsimd.iota(channel[:, :], pattern=[[0, 1]], base=0, channel_multiplier=1,
                           allow_small_or_imprecise_dtypes=True).then_inc(consts, 1)

            pool.wait_ge(windows_known, 2)
            all_fit = pool.value_load(fits_i[0:1, 0:1], min_val=0, max_val=1)
            pool.wait_ge(table_pads, 32)
            pool.wait_ge(tables_out, 32)

            def met():
                pool.sem_inc(pool_waits, 1)

            def gather(n, s, j):
                nc.gpsimd.indirect_dma_start(
                    out=gath[s][:, j * F:(j + 1) * F], out_offset=None, in_=a_table[:, :],
                    in_offset=bass.IndirectOffsetOnAxis(ap=gidx_a[s][j][:, :], axis=0)).then_inc(a_in[s], 16)

            def add_b(n, s):
                with pool.If(all_fit == 0):
                    pool.wait_ge(a_in[s], 16 * TILES * (n + 1))
                    met()
                    for j in range(TILES):
                        nc.gpsimd.indirect_dma_start(
                            out=gath[s][:, j * F:(j + 1) * F], out_offset=None, in_=b_table[:, :],
                            in_offset=bass.IndirectOffsetOnAxis(ap=gidx_b[s][j][:, :], axis=0),
                            compute_op=ALU.add).then_inc(b_in[s], 16)
                with pool.Else():
                    pool.sem_inc(b_in[s], 16 * TILES)

            for c in range(LEAD):
                pool.wait_ge(gidx_made, c + 1)
                for j in range(TILES):
                    gather(0, c, j)
                add_b(0, c)

            def step(n, s, before, after):
                c = n * SLOTS + s
                ns, nn = (s + LEAD) % SLOTS, n + (s + LEAD) // SLOTS
                if after >= LEAD:
                    pool.wait_ge(gidx_made, c + LEAD + 1)
                    met()
                for j in range(TILES):
                    if after >= LEAD:
                        gather(nn, ns, j)
                    if j == 0:
                        pool.wait_ge(sidx_made, c + 1)
                        pool.wait_ge(sum_copied, c + 1)
                    if before or j >= ACCS:
                        pool.wait_ge(scattered[j % ACCS], after_scatters(c) + 16 * (j // ACCS))
                    met()
                    nc.gpsimd.indirect_dma_start(
                        out=acc[j % ACCS][:, :],
                        out_offset=bass.IndirectOffsetOnAxis(ap=sidx[s][j][:, :], axis=0),
                        in_=summed[s][:, j * F:(j + 1) * F], in_offset=None,
                        compute_op=ALU.add).then_inc(scattered[j % ACCS], 16)
                if after >= LEAD:
                    add_b(nn, ns)

            pool.wait_ge(zeroed, 16 * ACCS)
            chunk_rounds(pool, step)

        @block.scalar
        def _(act):
            act.dma_start(xs[:, :, :], x.rearrange("(p b) f -> p b f", b=NB)).then_inc(x_in, 16)
            act.dma_start(we1ab[:, 0:F], We1[0:F, :]).then_inc(weights_in, 16)
            act.dma_start(we1ab[:, F:2 * F], We1[F:2 * F, :]).then_inc(weights_in, 16)
            act.dma_start(we2[0:F, :], We2[:, :]).then_inc(weights_in, 16)
            act.dma_start(we2[F:F + 1, :], be2.rearrange("(a f) -> a f", a=1)).then_inc(weights_in, 16)
            act.dma_start(wn1[:, :, :], Wn1.rearrange("(t k) f -> k t f", t=2)).then_inc(weights_in, 16)
            act.dma_start(wn2[0:F, :], Wn2[:, :]).then_inc(weights_in, 16)
            act.dma_start(wn2[F:F + 1, :], bn2.rearrange("(a f) -> a f", a=1)).then_inc(weights_in, 16)
            act.dma_start(wa[:, :], Wa.rearrange("f a -> a f").to_broadcast([P, F])).then_inc(weights_in, 16)
            act.dma_start(ba_col[:, :], ba.rearrange("(a f) -> a f", a=1).to_broadcast([P, 1])).then_inc(weights_in, 16)
            act.dma_start(be1_col[:, :], be1.rearrange("(f a) -> f a", a=1)).then_inc(weights_in, 16)
            act.dma_start(bn1_col[:, :], bn1.rearrange("(f a) -> f a", a=1)).then_inc(weights_in, 16)
            for s in range(SLOTS):
                act.dma_start(window[s][WIN:WIN + 1, :], We1[2 * F:2 * F + 1, :]).then_inc(weights_in, 16)
            act.wait_ge(consts, 1)
            for k in range(ACCS):
                act.dma_start(acc[k].rearrange("r f -> (r f)").rearrange("(p q) -> p q", p=P),
                              zeros[:, :]).then_inc(zeroed, 16)
            act.wait_ge(var_made, 1)
            nc.scalar.activation(stat[:, 2, :], stat[:, 1, :], ACT.Sqrt).then_inc(std_made, 1)
            for g, blocks in enumerate(GROUPS):
                w = len(blocks) * NP
                act.wait_ge(hT_in_psum, g + 1)
                nc.scalar.copy(hT[:, blocks[0] * NP:blocks[0] * NP + w], zt[g % 2][0:F, 0:w]).then_inc(hT_taken, 1)
            for g, blocks in enumerate(GROUPS):
                act.wait_ge(ab_in_psum, g + 1)
                v = z2[g % 2][0:NP, 0:len(blocks) * 2 * F].rearrange("p (b t f) -> p b t f", t=2, f=F)
                nc.scalar.copy(a_out[:, blocks[0]:blocks[-1] + 1, :], v[:, :, 0, :])
                nc.scalar.copy(b_out[:, blocks[0]:blocks[-1] + 1, :], v[:, :, 1, :]).then_inc(ab_taken, 1)
            act.wait_ge(ab_taken, len(GROUPS))
            act.dma_start(a_table[0:NODES, :].rearrange("(p b) f -> p b f", b=NB), a_out[:, :, :]).then_inc(tables_out, 16)
            act.dma_start(b_table[0:NODES, :].rearrange("(p b) f -> p b f", b=NB), b_out[:, :, :]).then_inc(tables_out, 16)
            act.wait_ge(weights_in, LOADED_W)

            def sigmoid1(c, s):
                act.wait_ge(z1_made, c + 1)
                nc.scalar.activation(sig1[s % 2][:, :], z1[s % 2][0:F, :], ACT.Sigmoid,
                                     bias=be1_col[:, :]).then_inc(sig1_made, 1)

            sigmoid1(0, 0)

            def copy_sums(n, s, reused):
                c = n * SLOTS + s
                act.wait_ge(sum_made, c + 1)
                if reused:
                    for k in range(ACCS):
                        act.wait_ge(scattered[k], after_scatters(c + 2 - SLOTS))
                nc.scalar.copy(summed[s][:, :], zs[s % 2][:, 0:TILES * F]).then_inc(sum_copied, 1)

            def step(n, s, before, after):
                c = n * SLOTS + s
                d = s % 2
                if after:
                    sigmoid1(c + 1, s + 1)
                act.wait_ge(z2_made, c + 1)
                nc.scalar.activation(sig2[d][:, :, :].rearrange("p t f -> p (t f)"), z2[d][:, 0:TILES * F],
                                     ACT.Sigmoid).then_inc(sig2_made, 1)
                if before:
                    copy_sums(*previous(n, s), before >= SLOTS)
                act.wait_ge(logit_made, c + 1)
                nc.scalar.activation(att[d][:, :], logit[d][:, :], ACT.Sigmoid,
                                     bias=ba_col[:, :]).then_inc(att_made, 1)

            chunk_rounds(act, step)
            copy_sums(ROUNDS - 1, SLOTS - 1, True)

            for g, blocks in enumerate(GROUPS):
                o, w = blocks[0] * NP, len(blocks) * NP
                act.wait_ge(z3_made, g + 1)
                nc.scalar.activation(sig3[:, o:o + w], z2[g % 2][0:F, 0:w], ACT.Sigmoid,
                                     bias=bn1_col[:, :]).then_inc(sig3_made, 1)

        @block.vector
        def _(dve):
            seq = [0]

            def link(ins):
                seq[0] += 1
                ins.then_inc(dve_seq, 1)
                dve.wait_ge(dve_seq, seq[0])

            PAD = float(NODES)
            base = SPLIT
            nc.vector.memset(src_i[base:CHUNKS, :], NODES)
            nc.vector.memset(dst_i[base:CHUNKS, :], NODES).then_inc(padded, 1)
            nc.vector.memset(attr[base:CHUNKS, :, :], 0.0).then_inc(padded, 1)
            for d in range(2):
                nc.vector.memset(e1[d][F:F + 1, :], 1.0)
            nc.vector.memset(n1[F:F + 1, :], 1.0)

            dve.wait_ge(edges_in, 96)
            nc.vector.tensor_copy(dst_h[:, :], dst_i[:, :]).then_inc(rows_made, 1)
            nc.vector.tensor_copy(src_h[:, :], src_i[:, :]).then_inc(rows_made, 1)
            nc.vector.tensor_copy(src_f[:, :], src_i[:, :])
            link(nc.vector.tensor_copy(dst_f[:, :], dst_i[:, :]))
            link(nc.vector.tensor_scalar(dst_f[:, 1:CH], dst_f[:, 1:CH], dst_f[:, 0:1], None, ALU.subtract))
            link(nc.vector.tensor_scalar(attr2[:, :, 0], dst_f[:, :], (WIN - 1) / 2.0, None, ALU.subtract))
            link(nc.vector.tensor_reduce(spread[:, :], attr2[:, 1:CH, 0], axis=AX.X, op=ALU.max,
                                         apply_absolute_value=True))
            dve.wait_ge(consts, 4)
            nc.vector.tensor_scalar(diag[:, 0, :], ident[0:CHUNKS, 0:CHUNKS], dst_f[:, 0:1], None, ALU.mult)
            link(nc.vector.tensor_scalar(diag[:, 1, :], ident[0:CHUNKS, 0:CHUNKS], spread[:, 0:1], None, ALU.mult))
            link(nc.vector.tensor_copy(dst_f[:, 1:CH], dst_i[:, 1:CH]))
            dve.sem_inc(diag_made, 1)
            dve.wait_ge(attr_in, 48)
            link(nc.vector.tensor_tensor(attr2[:, :, :], attr[:, :, :], attr[:, :, :], ALU.mult))
            nc.vector.tensor_reduce(radial[:, :], attr2[:, :, :], axis=AX.X, op=ALU.add).then_inc(rows_made, 1)

            dve.wait_ge(x_in, 16)
            link(nc.vector.tensor_reduce(stat[:, 0, :], xs[:, :, :], axis=AX.X, op=ALU.add))
            link(nc.vector.tensor_scalar(stat[:, 0, :], stat[:, 0, :], 1.0 / F, None, ALU.mult))
            link(nc.vector.tensor_tensor(xc[:, :, :], xs[:, :, :],
                                         stat[:, 0, :].rearrange("p (b a) -> p b a", a=1).to_broadcast([NP, NB, F]),
                                         ALU.subtract))
            link(nc.vector.tensor_tensor(h[:, :, :], xc[:, :, :], xc[:, :, :], ALU.mult))
            link(nc.vector.tensor_reduce(stat[:, 3, :], h[:, :, :], axis=AX.X, op=ALU.add))
            nc.vector.tensor_scalar(stat[:, 1, :], stat[:, 3, :], 1.0 / F, EPS, ALU.mult, ALU.add).then_inc(var_made, 1)
            dve.wait_ge(var_made, 1)
            dve.wait_ge(std_made, 1)
            link(nc.vector.reciprocal(stat[:, 3, :], stat[:, 2, :]))
            link(nc.vector.tensor_tensor(stat[:, 4, :], stat[:, 3, :], stat[:, 3, :], ALU.mult))
            link(nc.vector.tensor_tensor(stat[:, 4, :], stat[:, 4, :], stat[:, 1, :], ALU.mult))
            link(nc.vector.tensor_scalar(stat[:, 4, :], stat[:, 4, :], -0.5, 1.5, ALU.mult, ALU.add))
            link(nc.vector.tensor_tensor(stat[:, 5, :], stat[:, 4, :], stat[:, 3, :], ALU.mult))
            link(nc.vector.tensor_tensor(h[:, :, :], xc[:, :, :],
                                         stat[:, 5, :].rearrange("p (b a) -> p b a", a=1).to_broadcast([NP, NB, F]),
                                         ALU.mult))
            nc.vector.tensor_scalar(h[:, :, :], h[:, :, :], 0.0, None, ALU.max).then_inc(h_made, 1)

            dve.wait_ge(spread_in_psum, 1)
            link(nc.vector.tensor_reduce(worst[:, :], z1[0][:, CHUNKS:2 * CHUNKS], axis=AX.X, op=ALU.max))
            link(nc.vector.tensor_scalar(fits[:, :], worst[:, :], (WIN - 1) / 2.0, None, ALU.is_le))
            nc.vector.tensor_copy(fits_i[0:1, 0:1], fits[0:1, 0:1]).then_inc(windows_known, 1)
            link(nc.vector.tensor_scalar(win_row[:, :], z1[0][:, 0:CHUNKS], channel[:, 0:1], 1.0, ALU.add, ALU.add))
            nc.vector.tensor_scalar(win_row[:, :], win_row[:, :], fits[:, 0:1], 1.0, ALU.mult,
                                    ALU.subtract).then_inc(windows_known, 1)
            for t, cols in enumerate((src_cols, dst_cols)):
                dve.wait_ge(cols_in_psum, t + 1)
                link(nc.vector.tensor_copy(cols[:, :, :].rearrange("p c t -> p t c"),
                                           zs[t][:, 0:TILES * CHUNKS].rearrange("p (t c) -> p t c", t=TILES)))
            link(nc.vector.tensor_scalar(to_spare[:, :, :].rearrange("p c t -> p (c t)"),
                                         src_cols[:, :, :].rearrange("p c t -> p (c t)"),
                                         channel[:, 0:1], -1.0, ALU.subtract, ALU.mult))
            link(nc.vector.tensor_scalar(to_spare[:, :, :].rearrange("p c t -> p (c t)"),
                                         to_spare[:, :, :].rearrange("p c t -> p (c t)"),
                                         float(SPARE), None, ALU.add))
            dve.wait_ge(weights_in, LOADED_W)
            dve.wait_ge(windows_known, 2)

            def gather_indices(c, s):
                for j in range(TILES):
                    nc.vector.tensor_copy(gidx_b[s][j][:, :], dst_cols[:, bass.ds(c, 1), j])
                    last = nc.vector.tensor_copy(gidx_a[s][j][:, :], src_cols[:, bass.ds(c, 1), j])
                last.then_inc(gidx_made, 1)

            def one_hot(n, s):
                c = n * SLOTS + s
                dve.wait_ge(dst_in[s], 16 * (n + 1))
                nc.vector.tensor_scalar(onehot[s][0:WIN, :], dst_bc[s][:, :], win_row[0:WIN, bass.ds(c, 1)], None,
                                        ALU.is_equal).then_inc(onehot_made, 1)

            def silu1(c, s):
                dve.wait_ge(sig1_made, c + 1)
                nc.vector.scalar_tensor_tensor(e1[s % 2][0:F, :], z1[s % 2][0:F, :], be1_col[:, 0:1],
                                               sig1[s % 2][:, :], ALU.add, ALU.mult).then_inc(e1_made, 1)

            for c in range(SLOTS):
                gather_indices(c, c)
            for c in range(3):
                one_hot(0, c)
            silu1(0, 0)

            def same_src(n, s):
                c = n * SLOTS + s
                d = s % 2
                dve.wait_ge(att_made, c + 1)
                for j in range(TILES):
                    last = nc.vector.tensor_scalar(same[d][:, j, :], src_bc[s][:, j * P:(j + 1) * P],
                                                   src_cols[:, bass.ds(c, 1), j], att[d][:, j:j + 1],
                                                   ALU.is_equal, ALU.mult)
                last.then_inc(same_made, 1)

            def step(n, s, before, after):
                c = n * SLOTS + s
                d = s % 2
                dve.wait_ge(src_in[s], 16 * (n + 1))
                for j in range(TILES):
                    last = nc.vector.scalar_tensor_tensor(
                        same_before[d][:, j, :], src_bc[s][:, j * P:(j + 1) * P], src_cols[:, bass.ds(c, 1), j],
                        earlier[:, :], ALU.is_equal, ALU.mult, accum_out=dup[:, j:j + 1])
                last.then_inc(dup_made, 1)
                if before:
                    same_src(*previous(n, s))
                if after:
                    silu1(c + 1, s + 1)
                dve.wait_ge(sig2_made, c + 1)
                nc.vector.tensor_tensor(e2[d][:, :, :].rearrange("p t f -> p (t f)"), z2[d][:, 0:TILES * F],
                                        sig2[d][:, :, :].rearrange("p t f -> p (t f)"), ALU.mult).then_inc(e2_made, 1)
                dve.wait_ge(dup_made, c + 1)
                nc.vector.scalar_tensor_tensor(shift[:, :], dup[:, :], 0.5,
                                               to_spare[:, bass.ds(c, 1), :].rearrange("p a t -> p (a t)"),
                                               ALU.is_gt, ALU.mult).then_inc(shift_made, 1)
                dve.wait_ge(e2_made, c + 1)
                nc.vector.tensor_tensor(ewa[d][:, :, :], e2[d][:, :, :],
                                        wa[:, :].rearrange("p (t f) -> p t f", t=1).to_broadcast([P, TILES, F]),
                                        ALU.mult).then_inc(ewa_made, 1)
                dve.wait_ge(shift_made, c + 1)
                if before >= SLOTS:
                    for k in range(ACCS):
                        dve.wait_ge(scattered[k], after_scatters(c + 1 - SLOTS))
                for j in range(TILES):
                    last = nc.vector.tensor_tensor(sidx[s][j][:, :], src_cols[:, bass.ds(c, 1), j],
                                                   shift[:, j:j + 1], ALU.add)
                last.then_inc(sidx_made, 1)
                dve.wait_ge(ewa_made, c + 1)
                nc.vector.tensor_reduce(logit[d][:, :], ewa[d][:, :, :], axis=AX.X, op=ALU.add).then_inc(logit_made, 1)
                if after >= 3:
                    one_hot(n + (s + 3) // SLOTS, (s + 3) % SLOTS)
                if after >= SLOTS:
                    gather_indices(c + SLOTS, s)

            chunk_rounds(dve, step)
            same_src(ROUNDS - 1, SLOTS - 1)

            dve.wait_ge(aggs_in, 16 * ACCS)
            for k in range(1, ACCS):
                last = nc.vector.tensor_tensor(aggs[0][:, :, :], aggs[0][:, :, :], aggs[k][:, :, :], ALU.add)
                if k + 1 < ACCS:
                    link(last)
            last.then_inc(agg_made, 1)
            for g, blocks in enumerate(GROUPS):
                o, w = blocks[0] * NP, len(blocks) * NP
                dve.wait_ge(aggT_in_psum, g + 1)
                nc.vector.tensor_copy(aggT[:, o:o + w], z1[g % 2][0:F, 0:w]).then_inc(aggT_taken, 1)
            for g, blocks in enumerate(GROUPS):
                o, w = blocks[0] * NP, len(blocks) * NP
                dve.wait_ge(sig3_made, g + 1)
                nc.vector.scalar_tensor_tensor(n1[0:F, o:o + w], z2[g % 2][0:F, 0:w], bn1_col[:, 0:1],
                                               sig3[:, o:o + w], ALU.add, ALU.mult).then_inc(n1_made, 1)
            for g, blocks in enumerate(GROUPS):
                dve.wait_ge(y_made, g + 1)
                nc.vector.tensor_tensor(result[:, blocks[0]:blocks[-1] + 1, :],
                                        BANKS[g][0:NP, 0:len(blocks) * F].rearrange("p (b f) -> p b f", f=F),
                                        xs[:, blocks[0]:blocks[-1] + 1, :], ALU.add).then_inc(result_made, 1)

        @block.tensor
        def _(pe):
            pe.wait_ge(diag_made, 1)
            pe.wait_ge(consts, 4)
            nc.tensor.matmul(z1[0][:, 0:2 * CHUNKS], ones[0:CHUNKS, :],
                             diag[:, :, :].rearrange("p a c -> p (a c)"), start=True, stop=True).then_inc(spread_in_psum, 1)
            for t, rows in enumerate((src_f, dst_f)):
                for j in range(TILES):
                    last = nc.tensor.matmul(zs[t][:, j * CHUNKS:(j + 1) * CHUNKS], rows[:, j * P:(j + 1) * P],
                                            ident[0:CHUNKS, 0:CHUNKS], start=True, stop=True)
                last.then_inc(cols_in_psum, 1)
            pe.wait_ge(h_made, 1)
            for g, blocks in enumerate(GROUPS):
                if g >= 2:
                    pe.wait_ge(hT_taken, g - 1)
                for i, b in enumerate(blocks):
                    last = nc.tensor.matmul(zt[g % 2][0:F, i * NP:(i + 1) * NP], h[:, b, :], ident[0:NP, 0:NP],
                                            start=True, stop=True)
                last.then_inc(hT_in_psum, 1)
            pe.wait_ge(weights_in, LOADED_W)
            for g, blocks in enumerate(GROUPS):
                pe.wait_ge(hT_taken, g + 1)
                if g >= 2:
                    pe.wait_ge(ab_taken, g - 1)
                for i, b in enumerate(blocks):
                    last = nc.tensor.matmul(z2[g % 2][0:NP, i * 2 * F:(i + 1) * 2 * F], hT[:, b * NP:(b + 1) * NP],
                                            we1ab[:, :], start=True, stop=True)
                last.then_inc(ab_in_psum, 1)
            pe.wait_ge(windows_known, 2)
            pe.wait_ge(ab_taken, len(GROUPS))

            def first_layer(n, s):
                c = n * SLOTS + s
                d = s % 2
                pe.wait_ge(onehot_made, c + 1)
                pe.wait_ge(win_in[s], 32 * (n + 1))
                nc.tensor.matmul(z1[d][0:F, :], window[s][:, :], onehot[s][:, :], start=True, stop=False)
                pe.wait_ge(a_in[s], 16 * TILES * (n + 1))
                pe.wait_ge(b_in[s], 16 * TILES * (n + 1))
                for j in range(TILES):
                    last = nc.tensor.matmul(z1[d][0:F, j * P:(j + 1) * P], gath[s][:, j * F:(j + 1) * F],
                                            ident[:, :], start=False, stop=(j == TILES - 1))
                last.then_inc(z1_made, 1)

            first_layer(0, 0)
            first_layer(0, 1)

            def sum_by_src(n, s):
                c = n * SLOTS + s
                d = s % 2
                pe.wait_ge(same_made, c + 1)
                for j in range(TILES):
                    last = nc.tensor.matmul(zs[d][:, j * F:(j + 1) * F], same[d][:, j, :], e2[d][:, j, :],
                                            start=True, stop=True)
                last.then_inc(sum_made, 1)

            def step(n, s, before, after):
                c = n * SLOTS + s
                d = s % 2
                pe.wait_ge(e1_made, c + 1)
                for j in range(TILES):
                    last = nc.tensor.matmul(z2[d][:, j * F:(j + 1) * F], e1[d][:, j * P:(j + 1) * P], we2[:, :],
                                            start=True, stop=True)
                last.then_inc(z2_made, 1)
                if before:
                    sum_by_src(*previous(n, s))
                if after >= 2:
                    first_layer(n + (s + 2) // SLOTS, (s + 2) % SLOTS)

            chunk_rounds(pe, step)
            sum_by_src(ROUNDS - 1, SLOTS - 1)

            pe.wait_ge(agg_made, 1)
            for g, blocks in enumerate(GROUPS):
                if g >= 2:
                    pe.wait_ge(aggT_taken, g - 1)
                for i, b in enumerate(blocks):
                    last = nc.tensor.matmul(z1[g % 2][0:F, i * NP:(i + 1) * NP], aggs[0][:, b, :],
                                            ident[0:NP, 0:NP], start=True, stop=True)
                last.then_inc(aggT_in_psum, 1)
            for g, blocks in enumerate(GROUPS):
                o, w = blocks[0] * NP, len(blocks) * NP
                pe.wait_ge(aggT_taken, g + 1)
                if g >= 2:
                    pe.wait_ge(n1_made, g - 1)
                nc.tensor.matmul(z2[g % 2][0:F, 0:w], wn1[:, 0, :], hT[:, o:o + w], start=True, stop=False)
                nc.tensor.matmul(z2[g % 2][0:F, 0:w], wn1[:, 1, :], aggT[:, o:o + w], start=False,
                                 stop=True).then_inc(z3_made, 1)
            pe.wait_ge(n1_made, len(GROUPS))
            for g, blocks in enumerate(GROUPS):
                for i, b in enumerate(blocks):
                    last = nc.tensor.matmul(BANKS[g][0:NP, i * F:(i + 1) * F], n1[:, b * NP:(b + 1) * NP], wn2[:, :],
                                            start=True, stop=True)
                last.then_inc(y_made, 1)


_INS = ['x', 'src', 'dst', 'edge_attr_3', 'L0_gnn_We1', 'L0_gnn_be1', 'L0_gnn_We2', 'L0_gnn_be2', 'L0_gnn_Wa',
        'L0_gnn_ba', 'L0_gnn_Wn1', 'L0_gnn_bn1', 'L0_gnn_Wn2', 'L0_gnn_bn2']


def kernel(**inputs):
    import numpy as _np
    import concourse.bacc as _bacc
    from concourse import mybir as _mybir
    from concourse.bass_utils import run_bass_kernel_spmd as _run

    nc = _bacc.Bacc("TRN2", target_bir_lowering=False, num_devices=1)
    arrays, args = {}, []
    for name in _INS:
        a = _np.ascontiguousarray(inputs[name])
        arrays[f"in_{name}_dram"] = a
        args.append(nc.dram_tensor(f"in_{name}_dram", a.shape, _mybir.dt.from_np(a.dtype), kind="ExternalInput").ap())
    args.append(nc.dram_tensor("out_dram", inputs['x'].shape, _mybir.dt.float32, kind="ExternalOutput").ap())
    graph_layer(nc, *args)
    r = _run(nc, [arrays], core_ids=[0])
    return r.results[0]["out_dram"]
```

```python
import concourse.bass as bass
from concourse import mybir
from contextlib import ExitStack
import math


def graph_layer(nc, x, src, dst, edge_attr, We1, be1, We2, be2, Wa, ba, Wn1, bn1, Wn2, bn2, out):
    f32 = mybir.dt.float32
    i32 = mybir.dt.int32
    u32 = mybir.dt.uint32
    i16 = mybir.dt.int16
    bf16 = mybir.dt.bfloat16
    ALU = mybir.AluOpType
    ACT = mybir.ActivationFunctionType
    AX = mybir.AxisListType

    NODES, F = x.shape
    EDGES = src.shape[0]
    P = 128
    TILES = 4
    CH = TILES * P
    CHUNKS = -(-EDGES // CH)
    FULL = EDGES // CH
    REST = EDGES - FULL * CH
    SLOTS = 8
    ROUNDS = CHUNKS // SLOTS
    LEAD = 7
    WIN = 112
    NP = 125
    NB = NODES // NP
    SPARE = 3136
    ROWS = SPARE + P
    ACCS = 2
    PER_ACC = TILES // ACCS
    EPS = 1e-5
    GROUP = 4
    GROUPS = [range(g, min(g + GROUP, NB)) for g in range(0, NB, GROUP)]
    PARTS = 3
    PF = PARTS * F
    DENSE = [2, 5, 7]
    DENSE_LEAD = 2
    EDGE_BASE = 3.0
    EARLY = 4
    SPLIT = 96
    assert NP * NB == NODES and ROUNDS * SLOTS == CHUNKS and CHUNKS <= P and FULL == CHUNKS - 1
    assert NODES + WIN <= ROWS and NODES < SPARE and (ROWS * F) % P == 0

    cuts = [len(DENSE) * NB * w // SLOTS for w in range(SLOTS + 1)]
    shares = [[(i, max(lo, i * NB) - i * NB, min(hi, (i + 1) * NB) - i * NB) for i in range(len(DENSE))
               if max(lo, i * NB) < min(hi, (i + 1) * NB)] for lo, hi in zip(cuts, cuts[1:])]
    SHARE = max(hi - lo for lo, hi in zip(cuts, cuts[1:]))
    shares_before = [sum(len(v) for v in shares[:w]) for w in range(SLOTS + 1)]
    assert DENSE[0] >= DENSE_LEAD
    assert all(hi < NB or w == DENSE[i] for w in range(SLOTS) for i, lo, hi in shares[w])
    tiles_gathered = [(s, j) for s in range(SLOTS) if s not in DENSE for j in range(TILES)]
    cuts = [-(-len(tiles_gathered) * w // SLOTS) for w in range(SLOTS + 1)]
    gathers = [tiles_gathered[lo:hi] for lo, hi in zip(cuts, cuts[1:])]
    assert all(s <= w for w in range(SLOTS) for s, j in gathers[w])

    ctx = ExitStack()
    with ctx:
        def sb(name, shape, dt=f32):
            return ctx.enter_context(nc.sbuf_tensor(name, shape, dt))

        def pb(name, shape):
            return ctx.enter_context(nc.psum_tensor(name, shape, f32))

        def sem(name):
            return ctx.enter_context(nc.semaphore(name))

        def dram(name, shape, dt=f32):
            return nc.dram_tensor(name, shape, dt, kind="Internal").ap()

        a_table = dram("a_table", [ROWS, PF], bf16)
        b_table = dram("b_table", [ROWS, PF], bf16)
        acc = [dram(f"acc{k}", [ROWS, F]) for k in range(ACCS)]
        src_rows = dram("src_rows", [CHUNKS, CH], i16)
        dst_rows = dram("dst_rows", [CHUNKS, CH], i16)
        radial_rows = dram("radial_rows", [CHUNKS, PARTS * PARTS, CH], bf16)
        w_radial_rows = dram("w_radial_rows", [PARTS, F], bf16)

        ident = sb("ident", [P, P])
        ident_bf = sb("ident_bf", [P, P], bf16)
        ones = sb("ones", [P, P])
        table_loaded = sb("table_loaded", [NP, 1])
        weight = sb("weight", [P, 1])
        limit = sb("limit", [P, 1])
        channel = sb("channel", [P, 1])
        node_of = sb("node_of", [P, NB])
        zeros = sb("zeros", [P, ROWS * F // P])
        zeros_bf = zeros.bitcast(bf16)
        we1ab = sb("we1ab", [F, 2 * F])
        we2 = sb("we2", [F + 1, F])
        wn1 = sb("wn1", [2 * F, F])
        wn2 = sb("wn2", [F, F])
        bn2_all = sb("bn2_all", [NP, F])
        w_radial = sb("w_radial", [1, 2, F])
        w_radial3 = sb("w_radial3", [1, PARTS, F], bf16)
        w_radial9 = sb("w_radial9", [PARTS * PARTS, F], bf16)
        wa = sb("wa", [P, F])
        ba_col = sb("ba_col", [P, 1])
        be1_col = sb("be1_col", [F, 1])
        bn1_col = sb("bn1_col", [F, 1])

        xs = sb("xs", [NP, NB, F])
        xc = sb("xc", [NP, NB, F])
        h = sb("h", [NP, NB, F])
        stat = sb("stat", [NP, 6, NB])
        nodesT = sb("nodesT", [2 * F, NB * NP])
        hT = nodesT[0:F, :]
        a_parts = sb("a_parts", [P, NB, PARTS, F], bf16)
        b_parts = sb("b_parts", [P, NB, PARTS, F], bf16)
        ab_left = [sb(f"ab_left{g}", [NP, GROUP, 2, F]) for g in range(2)]

        arena = sb("arena", [P, 5888])
        free = [0]

        def part(columns, dt=f32):
            at = free[0]
            free[0] += columns
            v = arena[0:CHUNKS, at:at + columns]
            return v if dt is f32 else v.bitcast(dt)

        src_i = part(CH, i32)
        dst_i = part(CH, i32)
        src_f = part(CH)
        dst_f = part(CH)
        src_h = sb("src_h", [CHUNKS, CH], i16)
        dst_h = sb("dst_h", [CHUNKS, CH], i16)
        attr = part(3 * CH).rearrange("p (e k) -> p e k", k=3)
        attr2 = part(3 * CH).rearrange("p (e k) -> p e k", k=3)
        radial = part(CH)
        radial3 = sb("radial3", [CHUNKS, PARTS, CH], bf16)
        half = SHARE * CH // 2
        dense_onehot = [arena[0:NP, d * half:(d + 1) * half].bitcast(bf16).rearrange("p (b e) -> p b e", e=CH)
                        for d in range(2)]
        spread = sb("spread", [CHUNKS, 1])
        diag = sb("diag", [CHUNKS, 2, CHUNKS])
        src_cols = sb("src_cols", [P, CHUNKS, TILES])
        dst_cols = sb("dst_cols", [P, CHUNKS, TILES])
        to_spare = sb("to_spare", [P, CHUNKS, TILES])
        worst = sb("worst", [P, 1])
        fits = sb("fits", [P, 1])
        fits_i = sb("fits_i", [1, 1], i32)
        win_row = sb("win_row", [P, CHUNKS])

        src_bc = [sb(f"src_bc{s}", [P, CH], i16) for s in range(SLOTS)]
        dst_bc = [sb(f"dst_bc{s}", [WIN, CH], i16) for s in range(SLOTS)]
        window = [sb(f"window{s}", [WIN, PARTS, F], bf16) for s in range(SLOTS)]
        onehot = [sb(f"onehot{s}", [WIN, CH], bf16) for s in range(SLOTS)]
        radial9 = [sb(f"radial9_{s}", [PARTS * PARTS, CH], bf16) for s in range(SLOTS)]
        gath = [sb(f"gath{s}", [P, TILES * PF], bf16) for s in range(SLOTS)]
        dense_src = [sb(f"dense_src{i}", [NP, CH], i16) for i in range(len(DENSE))]
        gidx_a = [sb(f"gidx_a{s}", [P, TILES], u32) for s in range(SLOTS)]
        gidx_b = [sb(f"gidx_b{s}", [P, TILES], u32) for s in range(SLOTS)]
        sidx = [sb(f"sidx{s}", [P, TILES], u32) for s in range(SLOTS)]
        summed = [sb(f"summed{s}", [P, TILES, F + 1]) for s in range(SLOTS)]
        sig1 = [sb(f"sig1_{d}", [F, CH]) for d in range(2)]
        e1 = [sb(f"e1_{d}", [F + 1, CH]) for d in range(2)]
        sig2 = [sb(f"sig2_{d}", [P, TILES, F]) for d in range(2)]
        e2 = [sb(f"e2_{d}", [P, TILES, F]) for d in range(2)]
        ewa = [sb(f"ewa{d}", [P, TILES, F]) for d in range(2)]
        logit = [sb(f"logit{d}", [P, TILES]) for d in range(2)]
        att = [sb(f"att{d}", [P, TILES]) for d in range(2)]
        same = [sb(f"same{d}", [P, TILES, P]) for d in range(2)]
        message = [sb(f"message{d}", [P, TILES, F + 1]) for d in range(2)]
        shift = [sb(f"shift{d}", [P, TILES]) for d in range(2)]

        aggs = [v[0:NP, :, :, :].rearrange("p b k f -> p (b k f)").bitcast(f32)[:, 0:NB * F]
                .rearrange("p (b f) -> p b f", f=F) for v in (a_parts, b_parts)]
        sig3 = arena[0:F, 0:NB * NP]
        final = sb("final", [P, NB * NP])
        n1 = final[0:F, :]
        gath_b = [final[:, s * TILES * PF // 2:(s + 1) * TILES * PF // 2].bitcast(bf16) for s in range(SLOTS)]
        result = xc

        z1 = [pb(f"z1_{d}", [P, 512]) for d in range(2)]
        z2 = [pb(f"z2_{d}", [P, 512]) for d in range(2)]
        zs = [pb(f"zs_{d}", [P, 512]) for d in range(2)]
        zt = [pb(f"zt_{d}", [P, 512]) for d in range(2)]
        NODE_BANKS = [*z1, *z2, *zs, *zt]

        padded = sem("padded")
        attr_padded = sem("attr_padded")
        ones_made = sem("ones_made")
        zeros_made = sem("zeros_made")
        edges_in = sem("edges_in")
        attr_in = sem("attr_in")
        weights_in = sem("weights_in")
        x_in = sem("x_in")
        consts = sem("consts")
        dve_seq = sem("dve_seq")
        rows_made = sem("rows_made")
        rows_out = sem("rows_out")
        radial_out = sem("radial_out")
        cols_in_psum = sem("cols_in_psum")
        cols_taken = sem("cols_taken")
        diag_made = sem("diag_made")
        spread_in_psum = sem("spread_in_psum")
        windows_known = sem("windows_known")
        var_made = sem("var_made")
        std_made = sem("std_made")
        h_made = sem("h_made")
        hT_in_psum = sem("hT_in_psum")
        hT_taken = sem("hT_taken")
        ab_in_psum = sem("ab_in_psum")
        hi_made = sem("hi_made")
        left_made = sem("left_made")
        mid_made = sem("mid_made")
        parts_made = sem("parts_made")
        squares_made = sem("squares_made")
        radial_made = sem("radial_made")
        radial_hi = sem("radial_hi")
        radial_left = sem("radial_left")
        radial_mid = sem("radial_mid")
        w_row_in = sem("w_row_in")
        w_parts_made = sem("w_parts_made")
        w_rows_out = sem("w_rows_out")
        w_rows_in = sem("w_rows_in")
        table_pads = sem("table_pads")
        a_out = sem("a_out")
        b_out = sem("b_out")
        zeroed = sem("zeroed")
        src_in = [sem(f"src_in{s}") for s in range(SLOTS)]
        dst_in = [sem(f"dst_in{s}") for s in range(SLOTS)]
        win_in = [sem(f"win_in{s}") for s in range(SLOTS)]
        a_in = [sem(f"a_in{s}") for s in range(SLOTS)]
        dense_in = [sem(f"dense_in{i}") for i in range(len(DENSE))]
        dense_made = sem("dense_made")
        dense_used = sem("dense_used")
        dense_copied = sem("dense_copied")
        b_in = [sem(f"b_in{s}") for s in range(SLOTS)]
        gidx_made = sem("gidx_made")
        pool_waits = sem("pool_waits")
        onehot_made = sem("onehot_made")
        z1_made = sem("z1_made")
        sig1_made = sem("sig1_made")
        e1_made = sem("e1_made")
        z2_made = sem("z2_made")
        sig2_made = sem("sig2_made")
        e2_made = sem("e2_made")
        ewa_made = sem("ewa_made")
        logit_made = sem("logit_made")
        att_made = sem("att_made")
        shift_made = sem("shift_made")
        message_made = sem("message_made")
        weight_made = sem("weight_made")
        sidx_made = sem("sidx_made")
        same_made = sem("same_made")
        sum_made = sem("sum_made")
        sum_copied = sem("sum_copied")
        scattered = [sem(f"scattered{k}") for k in range(ACCS)]
        aggs_in = [sem(f"aggs_in{k}") for k in range(2)]
        x_made = sem("x_made")
        agg_made = sem("agg_made")
        aggT_in_psum = sem("aggT_in_psum")
        aggT_taken = sem("aggT_taken")
        z3_made = sem("z3_made")
        sig3_made = sem("sig3_made")
        n1_made = sem("n1_made")
        y_made = sem("y_made")
        result_made = sem("result_made")
        result_out = sem("result_out")

        def after_scatters(c):
            return 16 * PER_ACC * c

        LOADED_W = 16 * 11

        def chunk_rounds(engine, step):
            for s in range(SLOTS):
                step(0, s, s, SLOTS)
            with engine.Fori(1, ROUNDS - 1) as n:
                for s in range(SLOTS):
                    step(n, s, SLOTS, SLOTS)
            for s in range(SLOTS):
                step(ROUNDS - 1, s, SLOTS, SLOTS - 1 - s)

        def ab_psum(g):
            return zt[g % 2][0:NP, 0:len(GROUPS[g]) * 2 * F].rearrange("p (b t f) -> p b t f", t=2, f=F)

        def store_tables(engine, first, end):
            engine.wait_ge(parts_made, 2 * end)
            own = slice(GROUPS[first][0], GROUPS[end - 1][-1] + 1)
            for table, parts, done in ((a_table, a_parts, a_out), (b_table, b_parts, b_out)):
                engine.dma_start(table[0:NODES, :].rearrange("(p b) f -> p b f", b=NB)[:, own, :],
                                 parts[0:NP, own, :, :].rearrange("p b k f -> p b (k f)")).then_inc(done, 16)

        def ahead(n, s, steps):
            return n + (s + steps) // SLOTS, (s + steps) % SLOTS

        def parts_until(n, w):
            return n * shares_before[SLOTS] + shares_before[w]

        def previous(n, s):
            return (n, s - 1) if s else (n - 1, SLOTS - 1)

        block = ctx.enter_context(nc.Block())

        @block.sync
        def _(sp):
            sp.wait_ge(padded, 2)
            for flat, tile, done in ((dst, dst_i, edges_in), (src, src_i, edges_in)):
                v = flat[0:FULL * CH].rearrange("(c e) -> c e", e=CH)
                sp.dma_start(tile[0:SPLIT, :], v[0:SPLIT, :]).then_inc(done, 16)
                sp.dma_start(tile[SPLIT:FULL, :], v[SPLIT:FULL, :]).then_inc(done, 16)
                sp.dma_start(tile[FULL:CHUNKS, 0:REST],
                             flat[FULL * CH:EDGES].rearrange("(c e) -> c e", c=1)).then_inc(done, 16)
            sp.wait_ge(attr_padded, 1)
            v = edge_attr[0:FULL * CH, :].rearrange("(c e) k -> c e k", e=CH)
            sp.dma_start(attr[0:SPLIT, :, :], v[0:SPLIT, :, :]).then_inc(attr_in, 16)
            sp.dma_start(attr[SPLIT:FULL, :, :], v[SPLIT:FULL, :, :]).then_inc(attr_in, 16)
            sp.dma_start(attr[FULL:CHUNKS, 0:REST, :],
                         edge_attr[FULL * CH:EDGES, :].rearrange("(c e) k -> c e k", c=1)).then_inc(attr_in, 16)
            sp.wait_ge(zeros_made, 1)
            for table in (a_table, b_table):
                sp.dma_start(table[NODES:ROWS, :].rearrange("r f -> (r f)").rearrange("(p q) -> p q", p=F // 2),
                             zeros_bf[0:F // 2, 0:(ROWS - NODES) * PF // (F // 2)]).then_inc(table_pads, 16)
            sp.wait_ge(rows_made, 2)
            sp.dma_start(dst_rows[:, :], dst_h[:, :]).then_inc(rows_out, 16)
            sp.dma_start(src_rows[:, :], src_h[:, :]).then_inc(rows_out, 16)

            def store_radial():
                sp.wait_ge(rows_made, 3)
                sp.wait_ge(parts_made, 2 * len(GROUPS))
                v = radial_rows.rearrange("c (i j) e -> c i j e", j=PARTS)
                for j in range(PARTS):
                    sp.dma_start(v[:, :, j, :], radial3[:, :, :]).then_inc(radial_out, 16)

            def broadcast(rows, c, n):
                return rows[bass.ds(c, 1), :].to_broadcast([n, CH])

            def load_rows(c, s):
                sp.dma_start(dst_bc[s][:, :], broadcast(dst_rows, c, WIN)).then_inc(dst_in[s], 16)
                sp.dma_start(src_bc[s][:, :], broadcast(src_rows, c, P)).then_inc(src_in[s], 16)

            def load_window(c, s):
                first = sp.value_load(dst[bass.ds(c * CH, 1)].rearrange("(a b) -> a b", a=1),
                                      min_val=0, max_val=NODES - 1)
                sp.dma_start(window[s].rearrange("p k f -> p (k f)"),
                             b_table[bass.ds(first, WIN), :]).then_inc(win_in[s], 16)
                sp.dma_start(radial9[s][:, :],
                             radial_rows[bass.ds(c, 1), :, :].rearrange("a q e -> (a q) e")).then_inc(win_in[s], 16)

            def load_dense(n, i):
                sp.dma_start(dense_src[i][:, :], broadcast(src_rows, n * SLOTS + DENSE[i], NP)).then_inc(dense_in[i], 16)

            sp.wait_ge(rows_out, 32)
            for i in range(len(DENSE)):
                load_dense(0, i)
            for s in range(SLOTS):
                load_rows(s, s)
            sp.wait_ge(w_parts_made, 1)
            sp.dma_start(w_radial_rows[:, :].rearrange("k f -> (k f)").rearrange("(a q) -> a q", a=1),
                         w_radial3[:, :, :].rearrange("a k f -> a (k f)")).then_inc(w_rows_out, 16)
            sp.wait_ge(w_rows_out, 16)
            for i in range(PARTS):
                sp.dma_start(w_radial9[PARTS * i:PARTS * (i + 1), :], w_radial_rows[:, :]).then_inc(w_rows_in, 16)
            store_tables(sp, 0, EARLY)
            store_radial()
            sp.wait_ge(radial_out, 16 * PARTS)
            sp.wait_ge(table_pads, 32)
            sp.wait_ge(b_out, 32)
            for s in range(SLOTS):
                load_window(s, s)

            with sp.Fori(0, ROUNDS - 1) as n:
                for s in range(SLOTS):
                    c = n * SLOTS + s
                    for i, slot in enumerate(DENSE):
                        if s == max(0, slot - 2):
                            sp.wait_ge(dense_made, n * SLOTS + slot + 1)
                            load_dense(n + 1, i)
                    sp.wait_ge(z1_made, c + 1)
                    sp.wait_ge(same_made, c + 1)
                    load_rows(c + SLOTS, s)
                    load_window(c + SLOTS, s)

            halves = [(0, EARLY), (EARLY, len(GROUPS))]
            for half, (first, end) in enumerate(halves):
                own = slice(GROUPS[first][0], GROUPS[end - 1][-1] + 1)
                for k in range(ACCS):
                    sp.wait_ge(scattered[k], after_scatters(CHUNKS))
                    sp.dma_start(aggs[k][:, own, :], acc[k][0:NODES, :].rearrange("(p b) f -> p b f", b=NB)[:, own, :]
                                 ).then_inc(aggs_in[half], 16)
            for first, end in halves:
                own = slice(GROUPS[first][0], GROUPS[end - 1][-1] + 1)
                sp.wait_ge(result_made, end)
                sp.dma_start(out.rearrange("(p b) f -> p b f", b=NB)[:, own, :], result[:, own, :]).then_inc(result_out, 16)
            sp.wait_ge(result_out, 32)

        @block.gpsimd
        def _(pool):
            nc.gpsimd.memset(ones[:, :], 1.0).then_inc(ones_made, 1)
            pool.wait_ge(ones_made, 1)
            nc.gpsimd.affine_select(out=ident[:, :], in_=ones[:, :], compare_op=ALU.is_equal, fill=0.0,
                                    base=0, pattern=[[-1, P]], channel_multiplier=1).then_inc(consts, 1)
            nc.gpsimd.iota(channel[:, :], pattern=[[0, 1]], base=0, channel_multiplier=1,
                           allow_small_or_imprecise_dtypes=True).then_inc(consts, 1)
            nc.gpsimd.iota(node_of[:, :], pattern=[[1, NB]], base=0, channel_multiplier=NB,
                           allow_small_or_imprecise_dtypes=True).then_inc(consts, 1)
            pool.wait_ge(consts, 3)
            nc.gpsimd.tensor_copy(ident_bf[:, :], ident[:, :]).then_inc(consts, 1)

            pool.wait_ge(windows_known, 2)
            all_fit = pool.value_load(fits_i[0:1, 0:1], min_val=0, max_val=1)
            pool.wait_ge(table_pads, 32)
            pool.wait_ge(a_out, 32)

            def met():
                pool.sem_inc(pool_waits, 1)

            def gather(s, j):
                nc.gpsimd.indirect_dma_start(
                    out=gath[s][:, j * PF:(j + 1) * PF], out_offset=None, in_=a_table[:, :],
                    in_offset=bass.IndirectOffsetOnAxis(ap=gidx_a[s][:, j:j + 1], axis=0)).then_inc(a_in[s], 16)

            def gather_b(s):
                with pool.If(all_fit == 0):
                    pool.wait_ge(b_out, 32)
                    for j in range(TILES):
                        nc.gpsimd.indirect_dma_start(
                            out=gath_b[s][:, j * PF:(j + 1) * PF], out_offset=None, in_=b_table[:, :],
                            in_offset=bass.IndirectOffsetOnAxis(ap=gidx_b[s][:, j:j + 1], axis=0),
                        ).then_inc(b_in[s], 16)
                with pool.Else():
                    pass

            for c in range(LEAD):
                pool.wait_ge(gidx_made, c + 1)
                for s, j in gathers[c]:
                    gather(s, j)
                gather_b(c)

            def step(n, s, before, after):
                c = n * SLOTS + s
                ns = (s + LEAD) % SLOTS
                if after >= LEAD:
                    pool.wait_ge(gidx_made, c + LEAD + 1)
                    met()
                for j in range(TILES):
                    if after >= LEAD and j in (0, 2):
                        gather(*gathers[ns][j // 2])
                    if j == 0:
                        pool.wait_ge(sidx_made, c + 1)
                        pool.wait_ge(sum_copied, c + 1)
                    if before or j >= ACCS:
                        pool.wait_ge(scattered[j % ACCS], after_scatters(c) + 16 * (j // ACCS))
                    met()
                    nc.gpsimd.indirect_dma_start(
                        out=acc[j % ACCS][:, :],
                        out_offset=bass.IndirectOffsetOnAxis(ap=sidx[s][:, j:j + 1], axis=0),
                        in_=summed[s][:, j, 0:F], in_offset=None,
                        compute_op=ALU.add).then_inc(scattered[j % ACCS], 16)
                if after >= LEAD:
                    for g in gathers[ns][2:]:
                        gather(*g)
                    gather_b(ns)

            pool.wait_ge(zeroed, 16 * ACCS)
            chunk_rounds(pool, step)

        @block.scalar
        def _(act):
            act.dma_start(xs[:, :, :], x.rearrange("(p b) f -> p b f", b=NB)).then_inc(x_in, 16)
            act.dma_start(w_radial[:, 0, :], We1[2 * F:2 * F + 1, :]).then_inc(w_row_in, 16)
            act.dma_start(we1ab[:, 0:F], We1[0:F, :]).then_inc(weights_in, 16)
            act.dma_start(we1ab[:, F:2 * F], We1[F:2 * F, :]).then_inc(weights_in, 16)
            act.dma_start(we2[0:F, :], We2[:, :]).then_inc(weights_in, 16)
            act.dma_start(we2[F:F + 1, :], be2.rearrange("(a f) -> a f", a=1)).then_inc(weights_in, 16)
            act.dma_start(wn1[:, :], Wn1[:, :]).then_inc(weights_in, 16)
            act.dma_start(wn2[:, :], Wn2[:, :]).then_inc(weights_in, 16)
            act.dma_start(bn2_all[:, :], bn2.rearrange("(a f) -> a f", a=1).to_broadcast([NP, F])).then_inc(weights_in, 16)
            act.dma_start(wa[:, :], Wa.rearrange("f a -> a f").to_broadcast([P, F])).then_inc(weights_in, 16)
            act.dma_start(ba_col[:, :], ba.rearrange("(a f) -> a f", a=1).to_broadcast([P, 1])).then_inc(weights_in, 16)
            act.dma_start(be1_col[:, :], be1.rearrange("(f a) -> f a", a=1)).then_inc(weights_in, 16)
            act.dma_start(bn1_col[:, :], bn1.rearrange("(f a) -> f a", a=1)).then_inc(weights_in, 16)
            act.wait_ge(weight_made, 1)
            nc.scalar.activation(weight[:, :], weight[:, :], ACT.Exp).then_inc(weight_made, 1)
            act.wait_ge(var_made, 1)
            nc.scalar.activation(stat[:, 2, :], stat[:, 1, :], ACT.Sqrt).then_inc(std_made, 1)
            act.wait_ge(std_made, 1)
            nc.scalar.activation(table_loaded[:, :], stat[:, 2, 0:1], ACT.Sigmoid)
            act.wait_ge(zeros_made, 1)
            for k in range(ACCS):
                act.dma_start(acc[k].rearrange("r f -> (r f)").rearrange("(p q) -> p q", p=P),
                              zeros[:, :]).then_inc(zeroed, 16)
            def take_hT(g):
                blocks = GROUPS[g]
                w = len(blocks) * NP
                act.wait_ge(hT_in_psum, g + 1)
                nc.scalar.copy(hT[:, blocks[0] * NP:blocks[0] * NP + w], zs[g % 2][0:F, 0:w]).then_inc(hT_taken, 1)

            def mid(g):
                blocks = GROUPS[g]
                act.wait_ge(left_made, g + 1)
                for t, parts in enumerate((a_parts, b_parts)):
                    last = nc.scalar.copy(parts[0:NP, blocks[0]:blocks[-1] + 1, 1, :],
                                          ab_left[g % 2][:, 0:len(blocks), t, :])
                last.then_inc(mid_made, 1)

            take_hT(0)
            for g, blocks in enumerate(GROUPS):
                if g + 1 < len(GROUPS):
                    take_hT(g + 1)
                act.wait_ge(ab_in_psum, g + 1)
                v = ab_psum(g)
                for t, parts in enumerate((a_parts, b_parts)):
                    last = nc.scalar.copy(parts[0:NP, blocks[0]:blocks[-1] + 1, 0, :], v[:, :, t, :])
                last.then_inc(hi_made, 1)
                if g:
                    mid(g - 1)
                if g == 2:
                    act.wait_ge(radial_made, 1)
                    nc.scalar.copy(radial3[:, 0, :], radial).then_inc(radial_hi, 1)
                if g == 4:
                    act.wait_ge(radial_left, 1)
                    nc.scalar.copy(radial3[:, 1, :], attr2[:, :, 0]).then_inc(radial_mid, 1)
            mid(len(GROUPS) - 1)
            store_tables(act, EARLY, len(GROUPS))
            act.wait_ge(weights_in, LOADED_W)

            def dense_copy(n, i):
                act.wait_ge(dense_used, parts_until(n, DENSE[i]) + 1)
                for j in range(0, TILES, 2):
                    last = nc.scalar.copy(gath[DENSE[i]][:, j * PF:(j + 2) * PF], zt[j // 2][:, 0:2 * PF])
                last.then_inc(dense_copied, 1)

            def dense_copies(n, w):
                if w in DENSE:
                    dense_copy(n, DENSE.index(w))

            def sigmoid1(c, s):
                act.wait_ge(z1_made, c + 1)
                nc.scalar.activation(sig1[s % 2][:, :], z1[s % 2][0:F, :], ACT.Sigmoid,
                                     bias=be1_col[:, :]).then_inc(sig1_made, 1)

            sigmoid1(0, 0)

            def copy_sums(n, s, reused):
                c = n * SLOTS + s
                act.wait_ge(sum_made, c + 1)
                if reused:
                    for k in range(ACCS):
                        act.wait_ge(scattered[k], after_scatters(c + 2 - SLOTS))
                nc.scalar.copy(summed[s].rearrange("p t f -> p (t f)"), zs[s % 2][:, 0:TILES * (F + 1)]).then_inc(sum_copied, 1)

            def step(n, s, before, after):
                c = n * SLOTS + s
                d = s % 2
                if after:
                    sigmoid1(c + 1, s + 1)
                act.wait_ge(z2_made, c + 1)
                nc.scalar.activation(sig2[d][:, :, :].rearrange("p t f -> p (t f)"), z2[d][:, 0:TILES * F],
                                     ACT.Sigmoid).then_inc(sig2_made, 1)
                if before:
                    copy_sums(*previous(n, s), before >= SLOTS)
                if after >= DENSE_LEAD:
                    dense_copies(*ahead(n, s, DENSE_LEAD))
                act.wait_ge(logit_made, c + 1)
                nc.scalar.activation(att[d][:, :], logit[d][:, :], ACT.Sigmoid,
                                     bias=ba_col[:, :]).then_inc(att_made, 1)
                act.wait_ge(att_made, c + 1)
                for j in range(TILES):
                    last = nc.scalar.mul(message[d][:, j, 0:F], e2[d][:, j, :], att[d][:, j:j + 1])
                last.then_inc(message_made, 1)

            chunk_rounds(act, step)
            copy_sums(ROUNDS - 1, SLOTS - 1, True)

            def take_aggT(g):
                o, w = GROUPS[g][0] * NP, len(GROUPS[g]) * NP
                act.wait_ge(aggT_in_psum, g + 1)
                nc.scalar.copy(nodesT[F:2 * F, o:o + w], NODE_BANKS[g][F:2 * F, 0:w]).then_inc(aggT_taken, 1)

            take_aggT(0)
            for g, blocks in enumerate(GROUPS):
                o, w = blocks[0] * NP, len(blocks) * NP
                if g + 1 < len(GROUPS):
                    take_aggT(g + 1)
                act.wait_ge(z3_made, g + 1)
                nc.scalar.activation(sig3[:, o:o + w], NODE_BANKS[g][0:F, 0:w], ACT.Sigmoid,
                                     bias=bn1_col[:, :]).then_inc(sig3_made, 1)

        @block.vector
        def _(dve):
            seq = [0]

            def link(ins):
                seq[0] += 1
                ins.then_inc(dve_seq, 1)
                dve.wait_ge(dve_seq, seq[0])

            nc.vector.memset(src_i[SPLIT:CHUNKS, :], NODES).then_inc(padded, 1)
            nc.vector.memset(dst_i[SPLIT:CHUNKS, :], NODES).then_inc(padded, 1)
            nc.vector.memset(attr[SPLIT:CHUNKS, :, :], 0.0).then_inc(attr_padded, 1)
            nc.vector.memset(zeros[:, :], 0.0).then_inc(zeros_made, 1)
            for d in range(2):
                nc.vector.memset(e1[d][F:F + 1, :], 1.0)

            dve.wait_ge(consts, 4)
            nc.vector.tensor_scalar(weight[:, :], channel[:, :], -math.log(EDGE_BASE), (P // 2 - 1) * math.log(EDGE_BASE),
                                    ALU.mult, ALU.add).then_inc(weight_made, 1)

            dve.wait_ge(x_in, 16)
            link(nc.vector.tensor_reduce(stat[:, 0, :], xs[:, :, :], axis=AX.X, op=ALU.add))
            link(nc.vector.tensor_scalar(stat[:, 0, :], stat[:, 0, :], 1.0 / F, None, ALU.mult))
            link(nc.vector.tensor_tensor(xc[:, :, :], xs[:, :, :],
                                         stat[:, 0, :].rearrange("p (b a) -> p b a", a=1).to_broadcast([NP, NB, F]),
                                         ALU.subtract))
            link(nc.vector.tensor_tensor(h[:, :, :], xc[:, :, :], xc[:, :, :], ALU.mult))
            link(nc.vector.tensor_reduce(stat[:, 3, :], h[:, :, :], axis=AX.X, op=ALU.add))
            nc.vector.tensor_scalar(stat[:, 1, :], stat[:, 3, :], 1.0 / F, EPS, ALU.mult, ALU.add).then_inc(var_made, 1)
            dve.wait_ge(var_made, 1)
            dve.wait_ge(std_made, 1)
            link(nc.vector.reciprocal(stat[:, 3, :], stat[:, 2, :]))
            link(nc.vector.tensor_tensor(stat[:, 4, :], stat[:, 3, :], stat[:, 3, :], ALU.mult))
            link(nc.vector.tensor_tensor(stat[:, 4, :], stat[:, 4, :], stat[:, 1, :], ALU.mult))
            link(nc.vector.tensor_scalar(stat[:, 4, :], stat[:, 4, :], -0.5, 1.5, ALU.mult, ALU.add))
            link(nc.vector.tensor_tensor(stat[:, 5, :], stat[:, 4, :], stat[:, 3, :], ALU.mult))
            for g, blocks in enumerate(GROUPS):
                own = slice(blocks[0], blocks[-1] + 1)
                nc.vector.scalar_tensor_tensor(
                    h[:, own, :], xc[:, own, :], 0.0,
                    stat[:, 5, own].rearrange("p (b a) -> p b a", a=1).to_broadcast([NP, len(blocks), F]),
                    ALU.max, ALU.mult).then_inc(h_made, 1)

            dve.wait_ge(weight_made, 2)
            nc.vector.tensor_scalar(limit[:, :], weight[:, :], 2.0, None, ALU.mult)
            for d in range(2):
                for j in range(TILES):
                    nc.vector.tensor_copy(message[d][:, j, F:F + 1], weight[:, :])

            dve.wait_ge(edges_in, 96)
            nc.vector.tensor_copy(dst_h[:, :], dst_i).then_inc(rows_made, 1)
            nc.vector.tensor_copy(src_h[:, :], src_i).then_inc(rows_made, 1)
            nc.vector.tensor_copy(src_f, src_i)
            link(nc.vector.tensor_copy(dst_f, dst_i))
            link(nc.vector.tensor_scalar(dst_f[:, 1:CH], dst_f[:, 1:CH], dst_f[:, 0:1], None, ALU.subtract))
            link(nc.vector.tensor_scalar(radial, dst_f, (WIN - 1) / 2.0, None, ALU.subtract))
            link(nc.vector.tensor_reduce(spread[:, :], radial[:, 1:CH], axis=AX.X, op=ALU.max,
                                         apply_absolute_value=True))
            dve.wait_ge(consts, 4)
            nc.vector.tensor_scalar(diag[:, 0, :], ident[0:CHUNKS, 0:CHUNKS], dst_f[:, 0:1], None, ALU.mult)
            link(nc.vector.tensor_scalar(diag[:, 1, :], ident[0:CHUNKS, 0:CHUNKS], spread[:, 0:1], None, ALU.mult))
            nc.vector.tensor_copy(dst_f[:, 1:CH], dst_i[:, 1:CH]).then_inc(diag_made, 1)

            dve.wait_ge(w_row_in, 16)
            link(nc.vector.tensor_copy(w_radial3[:, 0, :], w_radial[:, 0, :]))
            link(nc.vector.tensor_tensor(w_radial[:, 1, :], w_radial[:, 0, :], w_radial3[:, 0, :], ALU.subtract))
            link(nc.vector.tensor_copy(w_radial3[:, 1, :], w_radial[:, 1, :]))
            nc.vector.tensor_tensor(w_radial3[:, 2, :], w_radial[:, 1, :], w_radial3[:, 1, :],
                                    ALU.subtract).then_inc(w_parts_made, 1)
            def radial_stage(g):
                if g == 0:
                    dve.wait_ge(attr_in, 48)
                    nc.vector.tensor_tensor(attr2, attr, attr, ALU.mult).then_inc(squares_made, 1)
                if g == 1:
                    dve.wait_ge(squares_made, 1)
                    nc.vector.tensor_reduce(radial, attr2, axis=AX.X, op=ALU.add).then_inc(radial_made, 1)
                if g == 3:
                    dve.wait_ge(radial_hi, 1)
                    nc.vector.tensor_tensor(attr2[:, :, 0], radial, radial3[:, 0, :],
                                            ALU.subtract).then_inc(radial_left, 1)
                if g == 5:
                    dve.wait_ge(radial_mid, 1)
                    nc.vector.tensor_tensor(radial3[:, 2, :], attr2[:, :, 0], radial3[:, 1, :],
                                            ALU.subtract).then_inc(rows_made, 1)

            def gather_indices(c, s):
                nc.vector.tensor_copy(gidx_b[s][:, :], dst_cols[:, bass.ds(c, 1), :].rearrange("p a t -> p (a t)"))
                nc.vector.tensor_copy(gidx_a[s][:, :],
                                      src_cols[:, bass.ds(c, 1), :].rearrange("p a t -> p (a t)")).then_inc(gidx_made, 1)

            def edge_columns():
                dve.wait_ge(spread_in_psum, 1)
                link(nc.vector.tensor_reduce(worst[:, :], z1[0][:, CHUNKS:2 * CHUNKS], axis=AX.X, op=ALU.max))
                link(nc.vector.tensor_scalar(fits[:, :], worst[:, :], (WIN - 1) / 2.0, None, ALU.is_le))
                nc.vector.tensor_copy(fits_i[0:1, 0:1], fits[0:1, 0:1]).then_inc(windows_known, 1)
                link(nc.vector.tensor_scalar(win_row[:, :], z1[0][:, 0:CHUNKS], channel[:, 0:1], 1.0, ALU.add, ALU.add))
                nc.vector.tensor_scalar(win_row[:, :], win_row[:, :], fits[:, 0:1], 1.0, ALU.mult,
                                        ALU.subtract).then_inc(windows_known, 1)
                for t, cols in enumerate((src_cols, dst_cols)):
                    dve.wait_ge(cols_in_psum, t + 1)
                    link(nc.vector.tensor_copy(cols[:, :, :].rearrange("p c t -> p t c"),
                                               z2[t][:, 0:TILES * CHUNKS].rearrange("p (t c) -> p t c", t=TILES)))
                link(nc.vector.tensor_scalar(to_spare[:, :, :].rearrange("p c t -> p (c t)"),
                                             src_cols[:, :, :].rearrange("p c t -> p (c t)"),
                                             channel[:, 0:1], -1.0, ALU.subtract, ALU.mult))
                link(nc.vector.tensor_scalar(to_spare[:, :, :].rearrange("p c t -> p (c t)"),
                                             to_spare[:, :, :].rearrange("p c t -> p (c t)"),
                                             float(SPARE), None, ALU.add))
                for c in range(SLOTS):
                    gather_indices(c, c)

            def low(g):
                blocks = GROUPS[g]
                dve.wait_ge(mid_made, g + 1)
                for t, parts in enumerate((a_parts, b_parts)):
                    own = parts[0:NP, blocks[0]:blocks[-1] + 1, :, :]
                    nc.vector.tensor_tensor(own[:, :, 2, :], ab_left[g % 2][:, 0:len(blocks), t, :], own[:, :, 1, :],
                                            ALU.subtract).then_inc(parts_made, 1)

            for g, blocks in enumerate(GROUPS):
                dve.wait_ge(hi_made, g + 1)
                if g >= 2:
                    dve.wait_ge(parts_made, 2 * (g - 1))
                for t, parts in enumerate((a_parts, b_parts)):
                    last = nc.vector.tensor_tensor(ab_left[g % 2][:, 0:len(blocks), t, :], ab_psum(g)[:, :, t, :],
                                                   parts[0:NP, blocks[0]:blocks[-1] + 1, 0, :], ALU.subtract)
                last.then_inc(left_made, 1)
                if g:
                    low(g - 1)
                radial_stage(g)
            low(len(GROUPS) - 1)
            edge_columns()

            dve.wait_ge(weights_in, LOADED_W)
            dve.wait_ge(windows_known, 2)

            def dense_one_hots(n, w):
                at = 0
                for i, lo, hi in shares[w]:
                    if lo == 0:
                        dve.wait_ge(dense_in[i], 16 * (n + 1))
                    for b in range(lo, hi):
                        last = nc.vector.tensor_scalar(dense_onehot[w % 2][:, at, :], dense_src[i][:, :],
                                                       node_of[0:NP, b:b + 1], None, ALU.is_equal)
                        at += 1
                last.then_inc(dense_made, 1)

            def one_hot(n, s):
                c = n * SLOTS + s
                dve.wait_ge(dst_in[s], 16 * (n + 1))
                nc.vector.tensor_scalar(onehot[s][:, :], dst_bc[s][:, :], win_row[0:WIN, bass.ds(c, 1)], None,
                                        ALU.is_equal).then_inc(onehot_made, 1)

            def silu1(c, s):
                dve.wait_ge(sig1_made, c + 1)
                nc.vector.scalar_tensor_tensor(e1[s % 2][0:F, :], z1[s % 2][0:F, :], be1_col[:, 0:1],
                                               sig1[s % 2][:, :], ALU.add, ALU.mult).then_inc(e1_made, 1)

            dve.wait_ge(rows_out, 32)
            dve.wait_ge(cols_in_psum, 2)
            for w in range(2):
                dense_one_hots(0, w)
            for c in range(3):
                one_hot(0, c)
            dve.wait_ge(dense_used, parts_until(0, DENSE_LEAD - 1))
            dense_one_hots(0, DENSE_LEAD)
            silu1(0, 0)

            def scatter_rows(n, s):
                c = n * SLOTS + s
                dve.wait_ge(sum_copied, c + 1)
                nc.vector.scalar_tensor_tensor(shift[s % 2][:, :], summed[s][:, :, F], limit[:, 0:1],
                                               to_spare[:, bass.ds(c, 1), :].rearrange("p a t -> p (a t)"),
                                               ALU.is_gt, ALU.mult).then_inc(shift_made, 1)
                dve.wait_ge(shift_made, c + 1)
                nc.vector.tensor_tensor(sidx[s][:, :], src_cols[:, bass.ds(c, 1), :].rearrange("p a t -> p (a t)"),
                                        shift[s % 2][:, :], ALU.add).then_inc(sidx_made, 1)

            def step(n, s, before, after):
                c = n * SLOTS + s
                d = s % 2
                dve.wait_ge(src_in[s], 16 * (n + 1))
                for j in range(TILES):
                    last = nc.vector.tensor_scalar(same[d][:, j, :], src_bc[s][:, j * P:(j + 1) * P],
                                                   src_cols[:, bass.ds(c, 1), j], None, ALU.is_equal)
                last.then_inc(same_made, 1)
                if after:
                    silu1(c + 1, s + 1)
                dve.wait_ge(sig2_made, c + 1)
                nc.vector.tensor_tensor(e2[d][:, :, :].rearrange("p t f -> p (t f)"), z2[d][:, 0:TILES * F],
                                        sig2[d][:, :, :].rearrange("p t f -> p (t f)"), ALU.mult).then_inc(e2_made, 1)
                dve.wait_ge(e2_made, c + 1)
                nc.vector.tensor_tensor(ewa[d][:, :, :], e2[d][:, :, :],
                                        wa[:, :].rearrange("p (t f) -> p t f", t=1).to_broadcast([P, TILES, F]),
                                        ALU.mult).then_inc(ewa_made, 1)
                if after >= 3:
                    one_hot(*ahead(n, s, 3))
                dve.wait_ge(ewa_made, c + 1)
                nc.vector.tensor_reduce(logit[d][:, :], ewa[d][:, :, :], axis=AX.X, op=ALU.add).then_inc(logit_made, 1)
                if before:
                    scatter_rows(*previous(n, s))
                if after > DENSE_LEAD:
                    dve.wait_ge(dense_used, parts_until(*ahead(n, s, DENSE_LEAD)))
                    dense_one_hots(*ahead(n, s, DENSE_LEAD + 1))
                if after >= SLOTS:
                    gather_indices(c + SLOTS, s)

            chunk_rounds(dve, step)
            scatter_rows(ROUNDS - 1, SLOTS - 1)

            nc.vector.tensor_tensor(xs[:, :, :], xs[:, :, :],
                                    bn2_all[:, :].rearrange("p (b f) -> p b f", b=1).to_broadcast([NP, NB, F]),
                                    ALU.add).then_inc(x_made, 1)
            dve.wait_ge(x_made, 1)
            for g, blocks in enumerate(GROUPS):
                own = slice(blocks[0], blocks[-1] + 1)
                dve.wait_ge(aggs_in[g // EARLY], 16 * ACCS)
                nc.vector.tensor_tensor(aggs[0][:, own, :], aggs[0][:, own, :], aggs[1][:, own, :],
                                        ALU.add).then_inc(agg_made, 1)

            def silu3(g):
                o, w = GROUPS[g][0] * NP, len(GROUPS[g]) * NP
                dve.wait_ge(sig3_made, g + 1)
                nc.vector.scalar_tensor_tensor(n1[:, o:o + w], NODE_BANKS[g][0:F, 0:w], bn1_col[:, 0:1],
                                               sig3[:, o:o + w], ALU.add, ALU.mult).then_inc(n1_made, 1)

            def add_x(g):
                own = slice(GROUPS[g][0], GROUPS[g][-1] + 1)
                dve.wait_ge(y_made, g + 1)
                nc.vector.tensor_tensor(result[:, own, :],
                                        NODE_BANKS[g][0:NP, 0:len(GROUPS[g]) * F].rearrange("p (b f) -> p b f", f=F),
                                        xs[:, own, :], ALU.add).then_inc(result_made, 1)

            for g in range(len(GROUPS)):
                silu3(g)
                if g:
                    add_x(g - 1)
            add_x(len(GROUPS) - 1)

        @block.tensor
        def _(pe):
            def edge_columns():
                pe.wait_ge(diag_made, 1)
                nc.tensor.matmul(z1[0][:, 0:2 * CHUNKS], ones[0:CHUNKS, :],
                                 diag[:, :, :].rearrange("p a c -> p (a c)"), start=True, stop=True).then_inc(spread_in_psum, 1)
                for t, rows in enumerate((src_f, dst_f)):
                    for j in range(TILES):
                        last = nc.tensor.matmul(z2[t][:, j * CHUNKS:(j + 1) * CHUNKS], rows[:, j * P:(j + 1) * P],
                                                ident[0:CHUNKS, 0:CHUNKS], start=True, stop=True)
                    last.then_inc(cols_in_psum, 1)

            pe.wait_ge(consts, 4)

            def h_transposed(g):
                pe.wait_ge(h_made, g + 1)
                if g >= 2:
                    pe.wait_ge(hT_taken, g - 1)
                for i, b in enumerate(GROUPS[g]):
                    last = nc.tensor.matmul(zs[g % 2][0:F, i * NP:(i + 1) * NP], h[:, b, :], ident[0:NP, 0:NP],
                                            start=True, stop=True)
                last.then_inc(hT_in_psum, 1)

            h_transposed(0)
            pe.wait_ge(weights_in, LOADED_W)
            for g, blocks in enumerate(GROUPS):
                if g + 1 < len(GROUPS):
                    h_transposed(g + 1)
                pe.wait_ge(hT_taken, g + 1)
                if g >= 2:
                    pe.wait_ge(left_made, g - 1)
                for i, b in enumerate(blocks):
                    last = nc.tensor.matmul(zt[g % 2][0:NP, i * 2 * F:(i + 1) * 2 * F],
                                            hT[:, b * NP:(b + 1) * NP], we1ab[:, :], start=True, stop=True)
                last.then_inc(ab_in_psum, 1)
                if g == 3:
                    edge_columns()
            pe.wait_ge(windows_known, 2)
            pe.wait_ge(parts_made, 2 * len(GROUPS))
            pe.wait_ge(w_rows_in, 16 * PARTS)
            all_fit = pe.value_load(fits_i[0:1, 0:1], min_val=0, max_val=1)

            def dense_products(n, w, part, opening=False):
                if part == len(shares[w]):
                    return
                i, lo, hi = shares[w][part]
                at = sum(end - start for _, start, end in shares[w][:part])
                if part == 0:
                    pe.wait_ge(dense_made, n * SLOTS + w + 1)
                if lo == 0 and (i or not opening):
                    pe.wait_ge(dense_copied, n * len(DENSE) + i)
                if lo == 0:
                    for bank in zt:
                        nc.tensor.matmul(bank[:, 0:2 * PF], zeros_bf[0:1, 0:P], zeros_bf[0:1, 0:2 * PF],
                                         start=True, stop=False)
                for b in range(lo, hi):
                    for j in range(TILES):
                        last = nc.tensor.matmul(zt[j // 2][:, j % 2 * PF:(j % 2 + 1) * PF],
                                                dense_onehot[w % 2][:, at + b - lo, j * P:(j + 1) * P],
                                                a_parts[0:NP, b, :, :].rearrange("p k f -> p (k f)"),
                                                start=False, stop=(b == NB - 1 and j % 2 == 1))
                last.then_inc(dense_used, 1)

            def picked(s, source, j, k):
                at = (j * PARTS + k) * F
                return nc.tensor.matmul(z1[s % 2][0:F, j * P:(j + 1) * P], source[:, at:at + F], ident_bf[:, :],
                                        start=False, stop=(source is gath[s] and j == TILES - 1 and k == PARTS - 1))

            def first_layer(n, s):
                c = n * SLOTS + s
                d = s % 2
                pe.wait_ge(onehot_made, c + 1)
                pe.wait_ge(win_in[s], 32 * (n + 1))
                for k in range(PARTS):
                    nc.tensor.matmul(z1[d][0:F, :], window[s][:, k, :], onehot[s][:, :], start=(k == 0), stop=False)
                nc.tensor.matmul(z1[d][0:F, :], w_radial9[:, :], radial9[s][:, :], start=False, stop=False)
                with pe.If(all_fit == 0):
                    pe.wait_ge(b_in[s], 16 * TILES * (n + 1))
                    for j in range(TILES):
                        for k in range(PARTS):
                            picked(s, gath_b[s], j, k)
                with pe.Else():
                    pass
                if s in DENSE:
                    pe.wait_ge(dense_copied, n * len(DENSE) + DENSE.index(s) + 1)
                else:
                    pe.wait_ge(a_in[s], 16 * TILES * (n + 1))
                for j in range(TILES):
                    for k in range(PARTS):
                        last = picked(s, gath[s], j, k)
                last.then_inc(z1_made, 1)

            for w in range(DENSE_LEAD):
                for part in range(2):
                    dense_products(0, w, part, opening=True)
            first_layer(0, 0)
            first_layer(0, 1)

            def sum_by_src(n, s):
                c = n * SLOTS + s
                d = s % 2
                pe.wait_ge(same_made, c + 1)
                pe.wait_ge(message_made, c + 1)
                for j in range(TILES):
                    last = nc.tensor.matmul(zs[d][:, j * (F + 1):(j + 1) * (F + 1)], same[d][:, j, :],
                                            message[d][:, j, :], start=True, stop=True)
                last.then_inc(sum_made, 1)

            def step(n, s, before, after):
                c = n * SLOTS + s
                d = s % 2
                pe.wait_ge(e1_made, c + 1)
                for j in range(TILES):
                    last = nc.tensor.matmul(z2[d][:, j * F:(j + 1) * F], e1[d][:, j * P:(j + 1) * P], we2[:, :],
                                            start=True, stop=True)
                last.then_inc(z2_made, 1)
                if before:
                    sum_by_src(*previous(n, s))
                if after >= DENSE_LEAD:
                    dense_products(*ahead(n, s, DENSE_LEAD), 0)
                if after >= 2:
                    first_layer(*ahead(n, s, 2))
                if after >= DENSE_LEAD:
                    dense_products(*ahead(n, s, DENSE_LEAD), 1)

            chunk_rounds(pe, step)
            sum_by_src(ROUNDS - 1, SLOTS - 1)

            def agg_transposed(g):
                pe.wait_ge(agg_made, g + 1)
                for i, b in enumerate(GROUPS[g]):
                    last = nc.tensor.matmul(NODE_BANKS[g][F:2 * F, i * NP:(i + 1) * NP], aggs[0][:, b, :],
                                            ident[0:NP, 0:NP], start=True, stop=True)
                last.then_inc(aggT_in_psum, 1)

            def second_product(g):
                pe.wait_ge(n1_made, g + 1)
                for i, b in enumerate(GROUPS[g]):
                    last = nc.tensor.matmul(NODE_BANKS[g][0:NP, i * F:(i + 1) * F], n1[:, b * NP:(b + 1) * NP],
                                            wn2[:, :], start=True, stop=True)
                last.then_inc(y_made, 1)

            pe.wait_ge(sum_copied, CHUNKS)
            pe.wait_ge(scattered[ACCS - 1], after_scatters(CHUNKS - 1))
            for g, blocks in enumerate(GROUPS):
                o, w = blocks[0] * NP, len(blocks) * NP
                nc.tensor.matmul(NODE_BANKS[g][0:F, 0:w], wn1[0:F, :], nodesT[0:F, o:o + w], start=True, stop=False)
            agg_transposed(0)
            for g, blocks in enumerate(GROUPS):
                o, w = blocks[0] * NP, len(blocks) * NP
                if g + 1 < len(GROUPS):
                    agg_transposed(g + 1)
                pe.wait_ge(aggT_taken, g + 1)
                nc.tensor.matmul(NODE_BANKS[g][0:F, 0:w], wn1[F:2 * F, :], nodesT[F:2 * F, o:o + w], start=False,
                                 stop=True).then_inc(z3_made, 1)
                if g:
                    second_product(g - 1)
            second_product(len(GROUPS) - 1)


_INS = ['x', 'src', 'dst', 'edge_attr_3', 'L0_gnn_We1', 'L0_gnn_be1', 'L0_gnn_We2', 'L0_gnn_be2', 'L0_gnn_Wa',
        'L0_gnn_ba', 'L0_gnn_Wn1', 'L0_gnn_bn1', 'L0_gnn_Wn2', 'L0_gnn_bn2']


def kernel(**inputs):
    import numpy as _np
    import concourse.bacc as _bacc
    from concourse import mybir as _mybir
    from concourse.bass_utils import run_bass_kernel_spmd as _run

    nc = _bacc.Bacc("TRN2", target_bir_lowering=False, num_devices=1)
    arrays, args = {}, []
    for name in _INS:
        a = _np.ascontiguousarray(inputs[name])
        arrays[f"in_{name}_dram"] = a
        args.append(nc.dram_tensor(f"in_{name}_dram", a.shape, _mybir.dt.from_np(a.dtype), kind="ExternalInput").ap())
    args.append(nc.dram_tensor("out_dram", inputs['x'].shape, _mybir.dt.float32, kind="ExternalOutput").ap())
    graph_layer(nc, *args)
    r = _run(nc, [arrays], core_ids=[0])
    return r.results[0]["out_dram"]
```

```python
import concourse.bass as bass
from concourse import mybir
from contextlib import ExitStack
import math


def graph_layer(nc, x, src, dst, edge_attr, We1, be1, We2, be2, Wa, ba, Wn1, bn1, Wn2, bn2, out):
    f32 = mybir.dt.float32
    i32 = mybir.dt.int32
    u32 = mybir.dt.uint32
    i16 = mybir.dt.int16
    bf16 = mybir.dt.bfloat16
    ALU = mybir.AluOpType
    ACT = mybir.ActivationFunctionType
    AX = mybir.AxisListType

    NODES, F = x.shape
    EDGES = src.shape[0]
    P = 128
    TILES = 4
    CH = TILES * P
    CHUNKS = -(-EDGES // CH)
    FULL = EDGES // CH
    REST = EDGES - FULL * CH
    SLOTS = 8
    ROUNDS = CHUNKS // SLOTS
    LEAD = 8
    WIN = 112
    NP = 125
    NB = NODES // NP
    SPARE = 3136
    ROWS = SPARE + P
    ACCS = 4
    PER_ACC = TILES // ACCS
    EPS = 1e-5
    GROUP = 4
    GROUPS = [range(g, min(g + GROUP, NB)) for g in range(0, NB, GROUP)]
    PARTS = 3
    PF = PARTS * F
    DENSE = [2, 5, 7]
    DENSE_LEAD = 2
    EDGE_BASE = 3.0
    PAIRS = -(-NB // 2)
    NODE_PAIRS = [range(q, min(q + 4, PAIRS)) for q in range(0, PAIRS, 4)]
    EARLY = 4
    SPLIT = 96
    NODE_BLOCKS = [slice(2 * v[0], min(2 * v[-1] + 2, NB)) for v in NODE_PAIRS]
    assert NP * NB == NODES and ROUNDS * SLOTS == CHUNKS and CHUNKS <= P and FULL == CHUNKS - 1
    assert NODES + WIN <= ROWS and NODES < SPARE and (ROWS * F) % P == 0

    cuts = [len(DENSE) * NB * w // SLOTS for w in range(SLOTS + 1)]
    shares = [[(i, max(lo, i * NB) - i * NB, min(hi, (i + 1) * NB) - i * NB) for i in range(len(DENSE))
               if max(lo, i * NB) < min(hi, (i + 1) * NB)] for lo, hi in zip(cuts, cuts[1:])]
    SHARE = max(hi - lo for lo, hi in zip(cuts, cuts[1:]))
    shares_before = [sum(len(v) for v in shares[:w]) for w in range(SLOTS + 1)]
    assert DENSE[0] >= DENSE_LEAD
    assert all(hi < NB or w == DENSE[i] for w in range(SLOTS) for i, lo, hi in shares[w])
    tiles_gathered = [(s, j) for s in range(SLOTS) if s not in DENSE for j in range(TILES)]
    cuts = [-(-len(tiles_gathered) * w // SLOTS) for w in range(SLOTS + 1)]
    gathers = [tiles_gathered[lo:hi] for lo, hi in zip(cuts, cuts[1:])]
    assert all(s <= w for w in range(SLOTS) for s, j in gathers[w])

    ctx = ExitStack()
    with ctx:
        def sb(name, shape, dt=f32):
            return ctx.enter_context(nc.sbuf_tensor(name, shape, dt))

        def pb(name, shape):
            return ctx.enter_context(nc.psum_tensor(name, shape, f32))

        def sem(name):
            return ctx.enter_context(nc.semaphore(name))

        def dram(name, shape, dt=f32):
            return nc.dram_tensor(name, shape, dt, kind="Internal").ap()

        a_table = dram("a_table", [ROWS, PF], bf16)
        b_table = dram("b_table", [ROWS, PF], bf16)
        acc = [dram(f"acc{k}", [ROWS, F]) for k in range(ACCS)]
        src_rows = dram("src_rows", [CHUNKS, CH], i16)
        dst_rows = dram("dst_rows", [CHUNKS, CH], i16)
        radial_rows = dram("radial_rows", [CHUNKS, PARTS * PARTS, CH], bf16)
        w_radial_rows = dram("w_radial_rows", [PARTS, PARTS * F], bf16)

        ident = sb("ident", [P, P])
        ident_bf = sb("ident_bf", [P, P], bf16)
        ones = sb("ones", [P, P])
        table_loaded = sb("table_loaded", [NP, 1])
        weight = sb("weight", [P, 1])
        limit = sb("limit", [P, 1])
        channel = sb("channel", [P, 1])
        node_of = sb("node_of", [P, NB])
        zeros = sb("zeros", [P, ROWS * F // P])
        zeros_bf = zeros.bitcast(bf16)
        we1ab = sb("we1ab", [2 * F, 2 * F])
        we2 = sb("we2", [F + 1, F])
        wn1 = sb("wn1", [2 * F, 2, 2 * F])
        wn2 = sb("wn2", [2 * F, 2 * F])
        bn2_all = sb("bn2_all", [NP, F])
        w_radial = sb("w_radial", [1, 2, F])
        w_radial3 = sb("w_radial3", [1, PARTS, F], bf16)
        wa = sb("wa", [P, F])
        ba_col = sb("ba_col", [P, 1])
        be1_col = sb("be1_col", [F, 1])
        bn1_col = sb("bn1_col", [2 * F, 1])

        xs = sb("xs", [NP, NB, F])
        xc = sb("xc", [NP, NB, F])
        h = sb("h", [NP, 2 * PAIRS, F])
        stat = sb("stat", [NP, 6, NB])
        hT = sb("hT", [2 * F, PAIRS * NP])
        ab_parts = sb("ab_parts", [P, 2, NB, PARTS, F], bf16)
        a_parts, b_parts = ab_parts[:, 0], ab_parts[:, 1]
        ab_left = [sb(f"ab_left{g}", [NP, GROUP, 2, F]) for g in range(2)]

        arena = sb("arena", [P, 5888])
        free = [0]

        def part(columns, dt=f32):
            at = free[0]
            free[0] += columns
            v = arena[0:CHUNKS, at:at + columns]
            return v if dt is f32 else v.bitcast(dt)

        src_i = part(CH, i32)
        dst_i = part(CH, i32)
        src_h = sb("src_h", [CHUNKS, CH], i16)
        dst_h = sb("dst_h", [CHUNKS, CH], i16)
        attr = part(3 * CH).rearrange("p (e k) -> p e k", k=3)
        assert free[0] >= SHARE * CH // 2
        src_f = part(CH)
        dst_f = part(CH)
        attr2 = part(3 * CH).rearrange("p (e k) -> p e k", k=3)
        radial = part(CH)
        radial3 = sb("radial3", [CHUNKS, PARTS, CH], bf16)
        half = SHARE * CH // 2
        dense_onehot = [arena[0:NP, d * half:(d + 1) * half].bitcast(bf16).rearrange("p (b e) -> p b e", e=CH)
                        for d in range(2)]
        spread = sb("spread", [CHUNKS, 1])
        diag = sb("diag", [CHUNKS, 2, CHUNKS])
        src_cols = sb("src_cols", [P, CHUNKS, TILES])
        dst_cols = sb("dst_cols", [P, CHUNKS, TILES])
        to_spare = sb("to_spare", [P, CHUNKS, TILES])
        worst = sb("worst", [P, 1])
        fits = sb("fits", [P, 1])
        fits_i = sb("fits_i", [1, 1], i32)
        win_row = sb("win_row", [P, CHUNKS])

        src_bc = [sb(f"src_bc{s}", [P, CH], i16) for s in range(SLOTS)]
        dst_bc = [sb(f"dst_bc{s}", [WIN, CH], i16) for s in range(SLOTS)]
        window = [sb(f"window{s}", [WIN + PARTS ** 2, PARTS, F], bf16) for s in range(SLOTS)]
        onehot = [sb(f"onehot{s}", [WIN + PARTS ** 2, CH], bf16) for s in range(SLOTS)]
        gath = [sb(f"gath{s}", [P, TILES * PF], bf16) for s in range(SLOTS)]
        dense_src = [sb(f"dense_src{i}", [NP, CH], i16) for i in range(len(DENSE))]
        gidx_a = [sb(f"gidx_a{s}", [P, TILES], u32) for s in range(SLOTS)]
        gidx_b = [sb(f"gidx_b{s}", [P, TILES], u32) for s in range(SLOTS)]
        sidx = [sb(f"sidx{s}", [P, TILES], u32) for s in range(SLOTS)]
        summed = [sb(f"summed{s}", [P, TILES, F + 1]) for s in range(SLOTS)]
        sig1 = [sb(f"sig1_{d}", [F, CH]) for d in range(2)]
        e1 = [sb(f"e1_{d}", [F + 1, CH]) for d in range(2)]
        sig2 = [sb(f"sig2_{d}", [P, TILES, F]) for d in range(2)]
        e2 = [sb(f"e2_{d}", [P, TILES, F]) for d in range(2)]
        ewa = [sb(f"ewa{d}", [P, TILES, F]) for d in range(2)]
        logit = [sb(f"logit{d}", [P, TILES]) for d in range(2)]
        att = [sb(f"att{d}", [P, TILES]) for d in range(2)]
        same = [sb(f"same{d}", [P, TILES, P]) for d in range(2)]
        message = [sb(f"message{d}", [P, TILES, F + 1]) for d in range(2)]
        shift = [sb(f"shift{d}", [P, TILES]) for d in range(2)]

        aggs = [v[0:NP, :, :, :].rearrange("p b k f -> p (b k f)").bitcast(f32)[:, 0:2 * PAIRS * F]
                .rearrange("p (b f) -> p b f", f=F) for v in (a_parts, b_parts)]
        aggs += [h, arena[0:NP, 2 * PAIRS * F:4 * PAIRS * F].rearrange("p (b f) -> p b f", f=F)]
        aggT = sb("aggT", [2 * F, PAIRS * NP])
        sig3 = arena[:, 0:PAIRS * NP]
        final = sb("final", [P, SLOTS * TILES * PF // 2])
        n1 = final[:, 0:PAIRS * NP]
        gath_b = [final[:, s * TILES * PF // 2:(s + 1) * TILES * PF // 2].bitcast(bf16) for s in range(SLOTS)]
        result = xc

        z1 = [pb(f"z1_{d}", [P, 512]) for d in range(2)]
        z2 = [pb(f"z2_{d}", [P, 512]) for d in range(2)]
        zs = [pb(f"zs_{d}", [P, 512]) for d in range(2)]
        zt = [pb(f"zt_{d}", [P, 512]) for d in range(2)]
        NODE_BANKS = [*z1, *z2]
        Y_BANKS = [*zs, *zt]

        padded = sem("padded")
        attr_padded = sem("attr_padded")
        ones_made = sem("ones_made")
        zeros_made = sem("zeros_made")
        edges_in = sem("edges_in")
        attr_in = sem("attr_in")
        weights_zeroed = sem("weights_zeroed")
        we1_in = sem("we1_in")
        weights_in = sem("weights_in")
        x_in = sem("x_in")
        consts = sem("consts")
        dve_seq = sem("dve_seq")
        rows_made = sem("rows_made")
        rows_out = sem("rows_out")
        radial_out = sem("radial_out")
        cols_in_psum = sem("cols_in_psum")
        diag_made = sem("diag_made")
        spread_in_psum = sem("spread_in_psum")
        windows_known = sem("windows_known")
        floats_made = sem("floats_made")
        var_made = sem("var_made")
        std_made = sem("std_made")
        h_made = sem("h_made")
        hT_in_psum = sem("hT_in_psum")
        hT_taken = sem("hT_taken")
        ab_in_psum = sem("ab_in_psum")
        hi_made = sem("hi_made")
        left_made = sem("left_made")
        mid_made = sem("mid_made")
        parts_made = sem("parts_made")
        squares_made = sem("squares_made")
        radial_made = sem("radial_made")
        radial_hi = sem("radial_hi")
        radial_left = sem("radial_left")
        radial_mid = sem("radial_mid")
        w_row_in = sem("w_row_in")
        w_parts_made = sem("w_parts_made")
        w_rows_out = sem("w_rows_out")
        w_rows_in = sem("w_rows_in")
        table_pads = sem("table_pads")
        a_out = sem("a_out")
        b_out = sem("b_out")
        zeroed = sem("zeroed")
        src_in = [sem(f"src_in{s}") for s in range(SLOTS)]
        dst_in = [sem(f"dst_in{s}") for s in range(SLOTS)]
        win_in = [sem(f"win_in{s}") for s in range(SLOTS)]
        a_in = [sem(f"a_in{s}") for s in range(SLOTS)]
        dense_in = [sem(f"dense_in{i}") for i in range(len(DENSE))]
        dense_made = sem("dense_made")
        dense_used = sem("dense_used")
        dense_copied = sem("dense_copied")
        b_in = [sem(f"b_in{s}") for s in range(SLOTS)]
        gidx_made = sem("gidx_made")
        pool_waits = sem("pool_waits")
        onehot_made = sem("onehot_made")
        z1_made = sem("z1_made")
        sig1_made = sem("sig1_made")
        e1_made = sem("e1_made")
        z2_made = sem("z2_made")
        sig2_made = sem("sig2_made")
        e2_made = sem("e2_made")
        ewa_made = sem("ewa_made")
        logit_made = sem("logit_made")
        att_made = sem("att_made")
        shift_made = sem("shift_made")
        message_made = sem("message_made")
        weight_made = sem("weight_made")
        sidx_made = sem("sidx_made")
        same_made = sem("same_made")
        sum_made = sem("sum_made")
        sum_copied = sem("sum_copied")
        scattered = [sem(f"scattered{k}") for k in range(ACCS)]
        aggs_in = [sem(f"aggs_in{g}") for g in range(len(NODE_PAIRS))]
        x_made = sem("x_made")
        agg_made = sem("agg_made")
        aggT_in_psum = sem("aggT_in_psum")
        aggT_taken = sem("aggT_taken")
        z3_made = sem("z3_made")
        sig3_made = sem("sig3_made")
        n1_made = sem("n1_made")
        y_made = sem("y_made")
        result_made = sem("result_made")
        result_out = sem("result_out")

        def after_scatters(c):
            return 16 * PER_ACC * c

        LOADED_W = 16 * 14

        def chunk_rounds(engine, step):
            for s in range(SLOTS):
                step(0, s, s, SLOTS)
            with engine.Fori(1, ROUNDS - 1) as n:
                for s in range(SLOTS):
                    step(n, s, SLOTS, SLOTS)
            for s in range(SLOTS):
                step(ROUNDS - 1, s, SLOTS, SLOTS - 1 - s)

        def ab_of_blocks(g, odd):
            count = len(GROUPS[g][odd::2])
            return ([zt, z2][odd][g % 2][0:NP, 0:count * 2 * F].rearrange("p (b t f) -> p b t f", t=2, f=F),
                    ab_left[g % 2][:, odd:len(GROUPS[g]):2, :, :])

        def part_of_blocks(g, k, odd=0, step=1):
            first, end = GROUPS[g][0] + odd, GROUPS[g][-1] + 1
            return ab_parts[0:NP, :, first:end:step, k, :].rearrange("p t b f -> p b t f")

        def pairs(g):
            return range(GROUPS[g][0] // 2, GROUPS[g][-1] // 2 + 1)

        def store_tables(engine, first, end):
            engine.wait_ge(parts_made, end)
            own = slice(GROUPS[first][0], GROUPS[end - 1][-1] + 1)
            for table, parts, done in ((a_table, a_parts, a_out), (b_table, b_parts, b_out)):
                engine.dma_start(table[0:NODES, :].rearrange("(p b) f -> p b f", b=NB)[:, own, :],
                                 parts[0:NP, own, :, :].rearrange("p b k f -> p b (k f)")).then_inc(done, 16)

        def ahead(n, s, steps):
            return n + (s + steps) // SLOTS, (s + steps) % SLOTS

        def parts_until(n, w):
            return n * shares_before[SLOTS] + shares_before[w]

        def previous(n, s):
            return (n, s - 1) if s else (n - 1, SLOTS - 1)

        block = ctx.enter_context(nc.Block())

        @block.sync
        def _(sp):
            sp.wait_ge(padded, 2)
            for flat, tile, done in ((dst, dst_i, edges_in), (src, src_i, edges_in)):
                v = flat[0:FULL * CH].rearrange("(c e) -> c e", e=CH)
                sp.dma_start(tile[0:SPLIT, :], v[0:SPLIT, :]).then_inc(done, 16)
                sp.dma_start(tile[SPLIT:FULL, :], v[SPLIT:FULL, :]).then_inc(done, 16)
                sp.dma_start(tile[FULL:CHUNKS, 0:REST],
                             flat[FULL * CH:EDGES].rearrange("(c e) -> c e", c=1)).then_inc(done, 16)
            sp.wait_ge(attr_padded, 1)
            v = edge_attr[0:FULL * CH, :].rearrange("(c e) k -> c e k", e=CH)
            sp.dma_start(attr[0:SPLIT, :, :], v[0:SPLIT, :, :]).then_inc(attr_in, 16)
            sp.dma_start(attr[SPLIT:FULL, :, :], v[SPLIT:FULL, :, :]).then_inc(attr_in, 16)
            sp.dma_start(attr[FULL:CHUNKS, 0:REST, :],
                         edge_attr[FULL * CH:EDGES, :].rearrange("(c e) k -> c e k", c=1)).then_inc(attr_in, 16)
            sp.wait_ge(weights_zeroed, 2)
            sp.dma_start(we2[0:F, :], We2[:, :]).then_inc(weights_in, 16)
            sp.dma_start(we2[F:F + 1, :], be2.rearrange("(a f) -> a f", a=1)).then_inc(weights_in, 16)
            for k in range(2):
                own = slice(k * F, (k + 1) * F)
                for half in range(2):
                    sp.dma_start(wn1[own, half, own], Wn1[half * F:(half + 1) * F, :]).then_inc(weights_in, 16)
                sp.dma_start(wn2[own, own], Wn2[:, :]).then_inc(weights_in, 16)
                sp.dma_start(bn1_col[own, :], bn1.rearrange("(f a) -> f a", a=1)).then_inc(weights_in, 16)
            sp.dma_start(bn2_all[:, :], bn2.rearrange("(a f) -> a f", a=1).to_broadcast([NP, F])).then_inc(weights_in, 16)
            sp.dma_start(wa[:, :], Wa.rearrange("f a -> a f").to_broadcast([P, F])).then_inc(weights_in, 16)
            sp.dma_start(ba_col[:, :], ba.rearrange("(a f) -> a f", a=1).to_broadcast([P, 1])).then_inc(weights_in, 16)
            sp.dma_start(be1_col[:, :], be1.rearrange("(f a) -> f a", a=1)).then_inc(weights_in, 16)
            sp.wait_ge(zeros_made, 1)
            for table in (a_table, b_table):
                sp.dma_start(table[NODES:ROWS, :].rearrange("r f -> (r f)").rearrange("(p q) -> p q", p=F // 2),
                             zeros_bf[0:F // 2, 0:(ROWS - NODES) * PF // (F // 2)]).then_inc(table_pads, 16)
            sp.wait_ge(rows_made, 2)
            sp.dma_start(dst_rows[:, :], dst_h[:, :]).then_inc(rows_out, 16)
            sp.dma_start(src_rows[:, :], src_h[:, :]).then_inc(rows_out, 16)

            def store_radial():
                sp.wait_ge(rows_made, 3)
                sp.wait_ge(parts_made, len(GROUPS))
                v = radial_rows.rearrange("c (i j) e -> c i j e", j=PARTS)
                for j in range(PARTS):
                    sp.dma_start(v[:, :, j, :], radial3[:, :, :]).then_inc(radial_out, 16)

            def broadcast(rows, c, n):
                return rows[bass.ds(c, 1), :].to_broadcast([n, CH])

            def load_rows(c, s):
                sp.dma_start(dst_bc[s][:, :], broadcast(dst_rows, c, WIN)).then_inc(dst_in[s], 16)
                sp.dma_start(src_bc[s][:, :], broadcast(src_rows, c, P)).then_inc(src_in[s], 16)

            def load_window(c, s):
                first = sp.value_load(dst[bass.ds(c * CH, 1)].rearrange("(a b) -> a b", a=1),
                                      min_val=0, max_val=NODES - 1)
                sp.dma_start(window[s][0:WIN].rearrange("p k f -> p (k f)"),
                             b_table[bass.ds(first, WIN), :]).then_inc(win_in[s], 16)
                sp.dma_start(onehot[s][WIN:WIN + PARTS ** 2, :],
                             radial_rows[bass.ds(c, 1), :, :].rearrange("a q e -> (a q) e")).then_inc(win_in[s], 16)

            def load_dense(n, i):
                sp.dma_start(dense_src[i][:, :], broadcast(src_rows, n * SLOTS + DENSE[i], NP)).then_inc(dense_in[i], 16)

            sp.wait_ge(w_parts_made, 1)
            for i in range(PARTS):
                sp.dma_start(w_radial_rows[i:i + 1, :],
                             w_radial3[:, :, :].rearrange("a k f -> a (k f)")).then_inc(w_rows_out, 16)
            sp.wait_ge(rows_out, 32)
            for i in range(len(DENSE)):
                load_dense(0, i)
            for s in range(SLOTS):
                load_rows(s, s)
            sp.wait_ge(w_rows_out, 16 * PARTS)
            for s in range(SLOTS):
                sp.dma_start(window[s][WIN:WIN + PARTS ** 2, 0, :],
                             w_radial_rows.rearrange("i (j f) -> (i j) f", f=F)).then_inc(w_rows_in, 16)
            store_radial()
            sp.wait_ge(radial_out, 16 * PARTS)
            sp.wait_ge(table_pads, 32)
            sp.wait_ge(b_out, 32)
            for s in range(SLOTS):
                load_window(s, s)

            with sp.Fori(0, ROUNDS - 1) as n:
                for s in range(SLOTS):
                    c = n * SLOTS + s
                    for i, slot in enumerate(DENSE):
                        if s == max(0, slot - 2):
                            sp.wait_ge(dense_made, n * SLOTS + slot + 1)
                            load_dense(n + 1, i)
                    sp.wait_ge(z1_made, c + 1)
                    sp.wait_ge(same_made, c + 1)
                    load_rows(c + SLOTS, s)
                    load_window(c + SLOTS, s)

            for k in range(ACCS):
                sp.wait_ge(scattered[k], after_scatters(CHUNKS))
            for g, own in enumerate(NODE_BLOCKS):
                for k in range(ACCS):
                    sp.dma_start(aggs[k][:, own, :], acc[k][0:NODES, :].rearrange("(p b) f -> p b f", b=NB)[:, own, :]
                                 ).then_inc(aggs_in[g], 16)
            for g, own in enumerate(NODE_BLOCKS):
                sp.wait_ge(result_made, g + 1)
                sp.dma_start(out.rearrange("(p b) f -> p b f", b=NB)[:, own, :], result[:, own, :]).then_inc(result_out, 16)
            sp.wait_ge(result_out, 16 * len(NODE_BLOCKS))

        @block.gpsimd
        def _(pool):
            nc.gpsimd.memset(ones[:, :], 1.0).then_inc(ones_made, 1)
            pool.wait_ge(ones_made, 1)
            nc.gpsimd.affine_select(out=ident[:, :], in_=ones[:, :], compare_op=ALU.is_equal, fill=0.0,
                                    base=0, pattern=[[-1, P]], channel_multiplier=1).then_inc(consts, 1)
            nc.gpsimd.iota(channel[:, :], pattern=[[0, 1]], base=0, channel_multiplier=1,
                           allow_small_or_imprecise_dtypes=True).then_inc(consts, 1)
            nc.gpsimd.iota(node_of[:, :], pattern=[[1, NB]], base=0, channel_multiplier=NB,
                           allow_small_or_imprecise_dtypes=True).then_inc(consts, 1)
            pool.wait_ge(consts, 3)
            nc.gpsimd.tensor_copy(ident_bf[:, :], ident[:, :]).then_inc(consts, 1)

            pool.wait_ge(edges_in, 96)
            nc.gpsimd.tensor_copy(dst_f, dst_i).then_inc(floats_made, 1)
            nc.gpsimd.tensor_copy(src_f, src_i).then_inc(floats_made, 1)
            pool.wait_ge(attr_in, 48)
            nc.gpsimd.tensor_tensor(attr2, attr, attr, ALU.mult).then_inc(squares_made, 1)
            pool.wait_ge(squares_made, 1)
            nc.gpsimd.tensor_tensor(radial, attr2[:, :, 0], attr2[:, :, 1], ALU.add).then_inc(squares_made, 1)
            pool.wait_ge(squares_made, 2)
            nc.gpsimd.tensor_tensor(radial, radial, attr2[:, :, 2], ALU.add).then_inc(radial_made, 1)

            pool.wait_ge(windows_known, 2)
            all_fit = pool.value_load(fits_i[0:1, 0:1], min_val=0, max_val=1)
            pool.wait_ge(table_pads, 32)
            pool.wait_ge(a_out, 32)

            def met():
                pool.sem_inc(pool_waits, 1)

            def gather(s, j):
                nc.gpsimd.indirect_dma_start(
                    out=gath[s][:, j * PF:(j + 1) * PF], out_offset=None, in_=a_table[:, :],
                    in_offset=bass.IndirectOffsetOnAxis(ap=gidx_a[s][:, j:j + 1], axis=0)).then_inc(a_in[s], 16)

            def gather_b(s):
                with pool.If(all_fit == 0):
                    pool.wait_ge(b_out, 32)
                    for j in range(TILES):
                        nc.gpsimd.indirect_dma_start(
                            out=gath_b[s][:, j * PF:(j + 1) * PF], out_offset=None, in_=b_table[:, :],
                            in_offset=bass.IndirectOffsetOnAxis(ap=gidx_b[s][:, j:j + 1], axis=0),
                        ).then_inc(b_in[s], 16)
                with pool.Else():
                    pass

            for c in range(LEAD):
                pool.wait_ge(gidx_made, c + 1)
                for s, j in gathers[c]:
                    gather(s, j)
                gather_b(c)

            def step(n, s, before, after):
                c = n * SLOTS + s
                ns = (s + LEAD) % SLOTS
                if after >= LEAD:
                    pool.wait_ge(gidx_made, c + LEAD + 1)
                    met()
                for j in range(TILES):
                    if after >= LEAD and j in (0, 2):
                        gather(*gathers[ns][j // 2])
                    if j == 0:
                        pool.wait_ge(sidx_made, c + 1)
                        pool.wait_ge(sum_copied, c + 1)
                    if before or j >= ACCS:
                        pool.wait_ge(scattered[j % ACCS], after_scatters(c) + 16 * (j // ACCS))
                    met()
                    nc.gpsimd.indirect_dma_start(
                        out=acc[j % ACCS][:, :],
                        out_offset=bass.IndirectOffsetOnAxis(ap=sidx[s][:, j:j + 1], axis=0),
                        in_=summed[s][:, j, 0:F], in_offset=None,
                        compute_op=ALU.add).then_inc(scattered[j % ACCS], 16)
                if after >= LEAD:
                    for g in gathers[ns][2:]:
                        gather(*g)
                    gather_b(ns)

            pool.wait_ge(zeroed, 16 * ACCS)
            chunk_rounds(pool, step)

        @block.scalar
        def _(act):
            act.dma_start(xs[:, :, :], x.rearrange("(p b) f -> p b f", b=NB)).then_inc(x_in, 16)
            act.dma_start(w_radial[:, 0, :], We1[2 * F:2 * F + 1, :]).then_inc(w_row_in, 16)
            for k in range(2):
                act.dma_start(we1ab[k * F:(k + 1) * F, 0:F], We1[0:F, :]).then_inc(we1_in, 16)
                act.dma_start(we1ab[k * F:(k + 1) * F, F:2 * F], We1[F:2 * F, :]).then_inc(we1_in, 16)
            act.wait_ge(zeros_made, 1)
            for k in range(ACCS):
                act.dma_start(acc[k].rearrange("r f -> (r f)").rearrange("(p q) -> p q", p=P),
                              zeros[:, :]).then_inc(zeroed, 16)
            act.wait_ge(var_made, 1)
            nc.scalar.activation(stat[:, 2, :], stat[:, 1, :], ACT.Sqrt).then_inc(std_made, 1)
            act.wait_ge(weight_made, 1)
            nc.scalar.activation(weight[:, :], weight[:, :], ACT.Exp).then_inc(weight_made, 1)
            act.wait_ge(std_made, 1)
            nc.scalar.activation(table_loaded[:, :], stat[:, 2, 0:1], ACT.Sigmoid)
            def take_hT(g):
                o, w = pairs(g)[0] * NP, len(pairs(g)) * NP
                act.wait_ge(hT_in_psum, g + 1)
                nc.scalar.copy(hT[:, o:o + w], zs[g % 2][:, 0:w]).then_inc(hT_taken, 1)

            def mid(g):
                act.wait_ge(left_made, g + 1)
                nc.scalar.copy(part_of_blocks(g, 1), ab_left[g % 2][:, 0:len(GROUPS[g]), :, :]).then_inc(mid_made, 1)

            take_hT(0)
            for g, blocks in enumerate(GROUPS):
                if g + 1 < len(GROUPS):
                    take_hT(g + 1)
                act.wait_ge(ab_in_psum, g + 1)
                for odd in range(min(2, len(blocks))):
                    last = nc.scalar.copy(part_of_blocks(g, 0, odd, 2), ab_of_blocks(g, odd)[0])
                last.then_inc(hi_made, 1)
                if g:
                    mid(g - 1)
                if g == 2:
                    act.wait_ge(radial_made, 1)
                    nc.scalar.copy(radial3[:, 0, :], radial).then_inc(radial_hi, 1)
                if g == 5:
                    store_tables(act, 0, EARLY)
                if g == 4:
                    act.wait_ge(radial_left, 1)
                    nc.scalar.copy(radial3[:, 1, :], attr2[:, :, 0]).then_inc(radial_mid, 1)
            mid(len(GROUPS) - 1)
            store_tables(act, EARLY, len(GROUPS))
            act.wait_ge(weights_in, LOADED_W)

            def dense_copy(n, i):
                act.wait_ge(dense_used, parts_until(n, DENSE[i]) + 1)
                for j in range(0, TILES, 2):
                    last = nc.scalar.copy(gath[DENSE[i]][:, j * PF:(j + 2) * PF], zt[j // 2][:, 0:2 * PF])
                last.then_inc(dense_copied, 1)

            def dense_copies(n, w):
                if w in DENSE:
                    dense_copy(n, DENSE.index(w))

            def sigmoid1(c, s):
                act.wait_ge(z1_made, c + 1)
                nc.scalar.activation(sig1[s % 2][:, :], z1[s % 2][0:F, :], ACT.Sigmoid,
                                     bias=be1_col[:, :]).then_inc(sig1_made, 1)

            sigmoid1(0, 0)

            def copy_sums(n, s, reused):
                c = n * SLOTS + s
                act.wait_ge(sum_made, c + 1)
                if reused:
                    for k in range(ACCS):
                        act.wait_ge(scattered[k], after_scatters(c + 2 - SLOTS))
                nc.scalar.copy(summed[s].rearrange("p t f -> p (t f)"), zs[s % 2][:, 0:TILES * (F + 1)]).then_inc(sum_copied, 1)

            def step(n, s, before, after):
                c = n * SLOTS + s
                d = s % 2
                if after:
                    sigmoid1(c + 1, s + 1)
                act.wait_ge(z2_made, c + 1)
                nc.scalar.activation(sig2[d][:, :, :].rearrange("p t f -> p (t f)"), z2[d][:, 0:TILES * F],
                                     ACT.Sigmoid).then_inc(sig2_made, 1)
                if before:
                    copy_sums(*previous(n, s), before >= SLOTS)
                if after >= DENSE_LEAD:
                    dense_copies(*ahead(n, s, DENSE_LEAD))
                act.wait_ge(logit_made, c + 1)
                nc.scalar.activation(att[d][:, :], logit[d][:, :], ACT.Sigmoid,
                                     bias=ba_col[:, :]).then_inc(att_made, 1)
                act.wait_ge(att_made, c + 1)
                for j in range(TILES):
                    last = nc.scalar.mul(message[d][:, j, 0:F], e2[d][:, j, :], att[d][:, j:j + 1])
                last.then_inc(message_made, 1)

            chunk_rounds(act, step)
            copy_sums(ROUNDS - 1, SLOTS - 1, True)

            def take_aggT(g):
                o, w = NODE_PAIRS[g][0] * NP, len(NODE_PAIRS[g]) * NP
                act.wait_ge(aggT_in_psum, g + 1)
                nc.scalar.copy(aggT[:, o:o + w], Y_BANKS[g][:, 0:w]).then_inc(aggT_taken, 1)

            take_aggT(0)
            for g, own in enumerate(NODE_PAIRS):
                o, w = own[0] * NP, len(own) * NP
                if g + 1 < len(NODE_PAIRS):
                    take_aggT(g + 1)
                act.wait_ge(z3_made, g + 1)
                nc.scalar.activation(sig3[:, o:o + w], NODE_BANKS[g][:, 0:w], ACT.Sigmoid,
                                     bias=bn1_col[:, :]).then_inc(sig3_made, 1)

        @block.vector
        def _(dve):
            seq = [0]

            def link(ins):
                seq[0] += 1
                ins.then_inc(dve_seq, 1)
                dve.wait_ge(dve_seq, seq[0])

            nc.vector.memset(src_i[SPLIT:CHUNKS, :], NODES).then_inc(padded, 1)
            nc.vector.memset(dst_i[SPLIT:CHUNKS, :], NODES).then_inc(padded, 1)
            nc.vector.memset(attr[SPLIT:CHUNKS, :, :], 0.0).then_inc(attr_padded, 1)
            nc.vector.memset(zeros[:, :], 0.0).then_inc(zeros_made, 1)
            nc.vector.memset(wn1[:, :, :], 0.0).then_inc(weights_zeroed, 1)
            nc.vector.memset(wn2[:, :], 0.0).then_inc(weights_zeroed, 1)
            nc.vector.memset(h[:, NB:2 * PAIRS, :], 0.0)
            for d in range(2):
                nc.vector.memset(e1[d][F:F + 1, :], 1.0)

            dve.wait_ge(consts, 4)
            nc.vector.tensor_scalar(weight[:, :], channel[:, :], -math.log(EDGE_BASE), (P // 2 - 1) * math.log(EDGE_BASE),
                                    ALU.mult, ALU.add).then_inc(weight_made, 1)

            dve.wait_ge(x_in, 16)
            link(nc.vector.tensor_reduce(stat[:, 0, :], xs[:, :, :], axis=AX.X, op=ALU.add))
            link(nc.vector.tensor_scalar(stat[:, 0, :], stat[:, 0, :], 1.0 / F, None, ALU.mult))
            link(nc.vector.tensor_tensor(xc[:, :, :], xs[:, :, :],
                                         stat[:, 0, :].rearrange("p (b a) -> p b a", a=1).to_broadcast([NP, NB, F]),
                                         ALU.subtract))
            link(nc.vector.tensor_tensor(h[:, 0:NB, :], xc[:, :, :], xc[:, :, :], ALU.mult))
            link(nc.vector.tensor_reduce(stat[:, 3, :], h[:, 0:NB, :], axis=AX.X, op=ALU.add))
            nc.vector.tensor_scalar(stat[:, 1, :], stat[:, 3, :], 1.0 / F, EPS, ALU.mult, ALU.add).then_inc(var_made, 1)
            dve.wait_ge(var_made, 1)
            dve.wait_ge(std_made, 1)
            link(nc.vector.reciprocal(stat[:, 3, :], stat[:, 2, :]))
            link(nc.vector.tensor_tensor(stat[:, 4, :], stat[:, 3, :], stat[:, 3, :], ALU.mult))
            link(nc.vector.tensor_tensor(stat[:, 4, :], stat[:, 4, :], stat[:, 1, :], ALU.mult))
            link(nc.vector.tensor_scalar(stat[:, 4, :], stat[:, 4, :], -0.5, 1.5, ALU.mult, ALU.add))
            link(nc.vector.tensor_tensor(stat[:, 5, :], stat[:, 4, :], stat[:, 3, :], ALU.mult))
            for g, blocks in enumerate(GROUPS):
                own = slice(blocks[0], blocks[-1] + 1)
                nc.vector.scalar_tensor_tensor(
                    h[:, own, :], xc[:, own, :], 0.0,
                    stat[:, 5, own].rearrange("p (b a) -> p b a", a=1).to_broadcast([NP, len(blocks), F]),
                    ALU.max, ALU.mult).then_inc(h_made, 1)

            dve.wait_ge(edges_in, 96)
            nc.vector.tensor_copy(dst_h[:, :], dst_i).then_inc(rows_made, 1)
            nc.vector.tensor_copy(src_h[:, :], src_i).then_inc(rows_made, 1)
            dve.wait_ge(floats_made, 1)
            offset = same[0][0:CHUNKS, :, :].rearrange("p t k -> p (t k)")
            link(nc.vector.tensor_scalar(offset, dst_i, dst_f[:, 0:1], (WIN - 1) / 2.0, ALU.subtract, ALU.subtract))
            link(nc.vector.tensor_reduce(spread[:, :], offset, axis=AX.X, op=ALU.max, apply_absolute_value=True))
            dve.wait_ge(consts, 4)
            nc.vector.tensor_scalar(diag[:, 0, :], ident[0:CHUNKS, 0:CHUNKS], dst_f[:, 0:1], None, ALU.mult)
            nc.vector.tensor_scalar(diag[:, 1, :], ident[0:CHUNKS, 0:CHUNKS], spread[:, 0:1], None,
                                    ALU.mult).then_inc(diag_made, 1)

            dve.wait_ge(w_row_in, 16)
            link(nc.vector.tensor_copy(w_radial3[:, 0, :], w_radial[:, 0, :]))
            link(nc.vector.tensor_tensor(w_radial[:, 1, :], w_radial[:, 0, :], w_radial3[:, 0, :], ALU.subtract))
            link(nc.vector.tensor_copy(w_radial3[:, 1, :], w_radial[:, 1, :]))
            nc.vector.tensor_tensor(w_radial3[:, 2, :], w_radial[:, 1, :], w_radial3[:, 1, :],
                                    ALU.subtract).then_inc(w_parts_made, 1)

            def radial_stage(g):
                if g == 3:
                    dve.wait_ge(radial_hi, 1)
                    nc.vector.tensor_tensor(attr2[:, :, 0], radial, radial3[:, 0, :],
                                            ALU.subtract).then_inc(radial_left, 1)
                if g == 5:
                    dve.wait_ge(radial_mid, 1)
                    nc.vector.tensor_tensor(radial3[:, 2, :], attr2[:, :, 0], radial3[:, 1, :],
                                            ALU.subtract).then_inc(rows_made, 1)

            def gather_indices(c, s):
                nc.vector.tensor_copy(gidx_b[s][:, :], dst_cols[:, bass.ds(c, 1), :].rearrange("p a t -> p (a t)"))
                nc.vector.tensor_copy(gidx_a[s][:, :],
                                      src_cols[:, bass.ds(c, 1), :].rearrange("p a t -> p (a t)")).then_inc(gidx_made, 1)

            def dense_one_hots(n, w, piece=0, pieces=1):
                matrices = [(i, b) for i, lo, hi in shares[w] for b in range(lo, hi)]
                cut = [len(matrices) * k // pieces for k in (piece, piece + 1)]
                for at in range(*cut):
                    i, b = matrices[at]
                    if b == 0:
                        dve.wait_ge(dense_in[i], 16 * (n + 1))
                    last = nc.vector.tensor_scalar(dense_onehot[w % 2][:, at, :], dense_src[i][:, :],
                                                   node_of[0:NP, b:b + 1], None, ALU.is_equal)
                if piece + 1 == pieces:
                    last.then_inc(dense_made, 1)

            def edge_columns():
                dve.wait_ge(spread_in_psum, 1)
                link(nc.vector.tensor_reduce(worst[:, :], z1[0][:, CHUNKS:2 * CHUNKS], axis=AX.X, op=ALU.max))
                link(nc.vector.tensor_scalar(fits[:, :], worst[:, :], (WIN - 1) / 2.0, None, ALU.is_le))
                nc.vector.tensor_copy(fits_i[0:1, 0:1], fits[0:1, 0:1]).then_inc(windows_known, 1)
                link(nc.vector.tensor_scalar(win_row[:, :], z1[0][:, 0:CHUNKS], channel[:, 0:1], 1.0, ALU.add, ALU.add))
                nc.vector.tensor_scalar(win_row[:, :], win_row[:, :], fits[:, 0:1], 1.0, ALU.mult,
                                        ALU.subtract).then_inc(windows_known, 1)
                for t, cols in enumerate((src_cols, dst_cols)):
                    dve.wait_ge(cols_in_psum, t + 1)
                    link(nc.vector.tensor_copy(cols[:, :, :].rearrange("p c t -> p t c"),
                                               [z1[1], zs[0]][t][:, 0:TILES * CHUNKS].rearrange("p (t c) -> p t c", t=TILES)))
                for c in range(4):
                    gather_indices(c, c)

            def low(g):
                dve.wait_ge(mid_made, g + 1)
                nc.vector.tensor_tensor(part_of_blocks(g, 2), ab_left[g % 2][:, 0:len(GROUPS[g]), :, :],
                                        part_of_blocks(g, 1), ALU.subtract).then_inc(parts_made, 1)

            for g, blocks in enumerate(GROUPS):
                dve.wait_ge(hi_made, g + 1)
                if g >= 2:
                    dve.wait_ge(parts_made, g - 1)
                for odd in range(min(2, len(blocks))):
                    in_psum, left = ab_of_blocks(g, odd)
                    last = nc.vector.tensor_tensor(left, in_psum, part_of_blocks(g, 0, odd, 2), ALU.subtract)
                last.then_inc(left_made, 1)
                if g:
                    low(g - 1)
                radial_stage(g)
                if g in (2, 3, 4):
                    dve.wait_ge(floats_made, 2)
                    dve.wait_ge(squares_made, 1)
                    dense_one_hots(0, 0, g - 2, 3)
            low(len(GROUPS) - 1)
            edge_columns()

            dve.wait_ge(weights_in, LOADED_W)
            dve.wait_ge(windows_known, 2)

            def one_hot(n, s):
                c = n * SLOTS + s
                dve.wait_ge(dst_in[s], 16 * (n + 1))
                nc.vector.tensor_scalar(onehot[s][0:WIN, :], dst_bc[s][:, :], win_row[0:WIN, bass.ds(c, 1)], None,
                                        ALU.is_equal).then_inc(onehot_made, 1)

            def silu1(c, s):
                dve.wait_ge(sig1_made, c + 1)
                nc.vector.scalar_tensor_tensor(e1[s % 2][0:F, :], z1[s % 2][0:F, :], be1_col[:, 0:1],
                                               sig1[s % 2][:, :], ALU.add, ALU.mult).then_inc(e1_made, 1)

            dve.wait_ge(cols_in_psum, 2)
            dense_one_hots(0, 1)
            for c in range(4, SLOTS):
                gather_indices(c, c)
            for c in range(3):
                one_hot(0, c)
            dve.wait_ge(weight_made, 2)
            nc.vector.tensor_scalar(limit[:, :], weight[:, :], 2.0, None, ALU.mult)
            for d in range(2):
                for j in range(TILES):
                    nc.vector.tensor_copy(message[d][:, j, F:F + 1], weight[:, :])
            link(nc.vector.tensor_scalar(to_spare[:, :, :].rearrange("p c t -> p (c t)"),
                                         src_cols[:, :, :].rearrange("p c t -> p (c t)"),
                                         channel[:, 0:1], -1.0, ALU.subtract, ALU.mult))
            link(nc.vector.tensor_scalar(to_spare[:, :, :].rearrange("p c t -> p (c t)"),
                                         to_spare[:, :, :].rearrange("p c t -> p (c t)"),
                                         float(SPARE), None, ALU.add))
            dve.wait_ge(dense_used, parts_until(0, DENSE_LEAD - 1))
            dense_one_hots(0, DENSE_LEAD)
            silu1(0, 0)

            def scatter_rows(n, s):
                c = n * SLOTS + s
                dve.wait_ge(sum_copied, c + 1)
                nc.vector.scalar_tensor_tensor(shift[s % 2][:, :], summed[s][:, :, F], limit[:, 0:1],
                                               to_spare[:, bass.ds(c, 1), :].rearrange("p a t -> p (a t)"),
                                               ALU.is_gt, ALU.mult).then_inc(shift_made, 1)
                dve.wait_ge(shift_made, c + 1)
                nc.vector.tensor_tensor(sidx[s][:, :], src_cols[:, bass.ds(c, 1), :].rearrange("p a t -> p (a t)"),
                                        shift[s % 2][:, :], ALU.add).then_inc(sidx_made, 1)

            def step(n, s, before, after):
                c = n * SLOTS + s
                d = s % 2
                dve.wait_ge(src_in[s], 16 * (n + 1))
                for j in range(TILES):
                    last = nc.vector.tensor_scalar(same[d][:, j, :], src_bc[s][:, j * P:(j + 1) * P],
                                                   src_cols[:, bass.ds(c, 1), j], None, ALU.is_equal)
                last.then_inc(same_made, 1)
                if after:
                    silu1(c + 1, s + 1)
                dve.wait_ge(sig2_made, c + 1)
                nc.vector.tensor_tensor(e2[d][:, :, :].rearrange("p t f -> p (t f)"), z2[d][:, 0:TILES * F],
                                        sig2[d][:, :, :].rearrange("p t f -> p (t f)"), ALU.mult).then_inc(e2_made, 1)
                dve.wait_ge(e2_made, c + 1)
                nc.vector.tensor_tensor(ewa[d][:, :, :], e2[d][:, :, :],
                                        wa[:, :].rearrange("p (t f) -> p t f", t=1).to_broadcast([P, TILES, F]),
                                        ALU.mult).then_inc(ewa_made, 1)
                if after >= 3:
                    one_hot(*ahead(n, s, 3))
                dve.wait_ge(ewa_made, c + 1)
                nc.vector.tensor_reduce(logit[d][:, :], ewa[d][:, :, :], axis=AX.X, op=ALU.add).then_inc(logit_made, 1)
                if before:
                    scatter_rows(*previous(n, s))
                if after > DENSE_LEAD:
                    dve.wait_ge(dense_used, parts_until(*ahead(n, s, DENSE_LEAD)))
                    dense_one_hots(*ahead(n, s, DENSE_LEAD + 1))
                if after >= SLOTS:
                    gather_indices(c + SLOTS, s)

            chunk_rounds(dve, step)
            scatter_rows(ROUNDS - 1, SLOTS - 1)

            nc.vector.tensor_tensor(xs[:, :, :], xs[:, :, :],
                                    bn2_all[:, :].rearrange("p (b f) -> p b f", b=1).to_broadcast([NP, NB, F]),
                                    ALU.add).then_inc(x_made, 1)
            nc.vector.memset(aggs[0][:, NB:2 * PAIRS, :], 0.0)
            dve.wait_ge(x_made, 1)
            def add_aggs(g):
                own = NODE_BLOCKS[g]
                dve.wait_ge(aggs_in[g], 16 * ACCS)
                for k, (to, of) in enumerate(((0, 1), (2, 3), (0, 2))):
                    last = nc.vector.tensor_tensor(aggs[to][:, own, :], aggs[to][:, own, :], aggs[of][:, own, :], ALU.add)
                    if k == 1:
                        link(last)
                last.then_inc(agg_made, 1)

            def silu3(g):
                o, w = NODE_PAIRS[g][0] * NP, len(NODE_PAIRS[g]) * NP
                dve.wait_ge(sig3_made, g + 1)
                nc.vector.scalar_tensor_tensor(n1[:, o:o + w], NODE_BANKS[g][:, 0:w], bn1_col[:, 0:1],
                                               sig3[:, o:o + w], ALU.add, ALU.mult).then_inc(n1_made, 1)

            def add_x(g):
                own = NODE_BLOCKS[g]
                n_own = own.stop - own.start
                dve.wait_ge(y_made, g + 1)
                nc.vector.tensor_tensor(result[:, own, :],
                                        Y_BANKS[g][0:NP, 0:n_own * F].rearrange("p (b f) -> p b f", f=F),
                                        xs[:, own, :], ALU.add).then_inc(result_made, 1)

            for g in range(2):
                add_aggs(g)
            for g in range(len(NODE_PAIRS)):
                if g + 2 < len(NODE_PAIRS):
                    add_aggs(g + 2)
                silu3(g)
                if g:
                    add_x(g - 1)
            add_x(len(NODE_PAIRS) - 1)

        @block.tensor
        def _(pe):
            def edge_columns():
                pe.wait_ge(diag_made, 1)
                nc.tensor.matmul(z1[0][:, 0:2 * CHUNKS], ones[0:CHUNKS, :],
                                 diag[:, :, :].rearrange("p a c -> p (a c)"), start=True, stop=True).then_inc(spread_in_psum, 1)
                pe.wait_ge(floats_made, 2)
                pe.wait_ge(hT_taken, len(GROUPS))
                for t, rows in enumerate((src_f, dst_f)):
                    for j in range(TILES):
                        last = nc.tensor.matmul([z1[1], zs[0]][t][:, j * CHUNKS:(j + 1) * CHUNKS], rows[:, j * P:(j + 1) * P],
                                                ident[0:CHUNKS, 0:CHUNKS], start=True, stop=True)
                    last.then_inc(cols_in_psum, 1)

            pe.wait_ge(consts, 4)

            def h_transposed(g):
                pe.wait_ge(h_made, g + 1)
                if g >= 2:
                    pe.wait_ge(hT_taken, g - 1)
                for i, q in enumerate(pairs(g)):
                    last = nc.tensor.matmul(zs[g % 2][:, i * NP:(i + 1) * NP],
                                            h[:, 2 * q:2 * q + 2, :].rearrange("p b f -> p (b f)"),
                                            ident[0:NP, 0:NP], start=True, stop=True)
                last.then_inc(hT_in_psum, 1)

            h_transposed(0)
            pe.wait_ge(we1_in, 64)
            for g, blocks in enumerate(GROUPS):
                if g + 1 < len(GROUPS):
                    h_transposed(g + 1)
                pe.wait_ge(hT_taken, g + 1)
                if g >= 2:
                    pe.wait_ge(left_made, g - 1)
                for i, b in enumerate(blocks):
                    last = nc.tensor.matmul([zt, z2][i % 2][g % 2][0:NP, i // 2 * 2 * F:(i // 2 + 1) * 2 * F],
                                            hT[b % 2 * F:(b % 2 + 1) * F, b // 2 * NP:(b // 2 + 1) * NP],
                                            we1ab[b % 2 * F:(b % 2 + 1) * F, :], start=True, stop=True)
                last.then_inc(ab_in_psum, 1)
            edge_columns()
            pe.wait_ge(windows_known, 2)
            pe.wait_ge(parts_made, len(GROUPS))
            pe.wait_ge(w_rows_in, 16 * SLOTS)
            all_fit = pe.value_load(fits_i[0:1, 0:1], min_val=0, max_val=1)

            def dense_products(n, w, part, opening=False):
                if part == len(shares[w]):
                    return
                i, lo, hi = shares[w][part]
                at = sum(end - start for _, start, end in shares[w][:part])
                if part == 0:
                    pe.wait_ge(dense_made, n * SLOTS + w + 1)
                if lo == 0 and (i or not opening):
                    pe.wait_ge(dense_copied, n * len(DENSE) + i)
                if lo == 0:
                    for bank in zt:
                        nc.tensor.matmul(bank[:, 0:2 * PF], zeros_bf[0:1, 0:P], zeros_bf[0:1, 0:2 * PF],
                                         start=True, stop=False)
                for b in range(lo, hi):
                    for j in range(TILES):
                        last = nc.tensor.matmul(zt[j // 2][:, j % 2 * PF:(j % 2 + 1) * PF],
                                                dense_onehot[w % 2][:, at + b - lo, j * P:(j + 1) * P],
                                                a_parts[0:NP, b, :, :].rearrange("p k f -> p (k f)"),
                                                start=False, stop=(b == NB - 1 and j % 2 == 1))
                last.then_inc(dense_used, 1)

            def picked(s, source, j, k):
                at = (j * PARTS + k) * F
                return nc.tensor.matmul(z1[s % 2][0:F, j * P:(j + 1) * P], source[:, at:at + F], ident_bf[:, :],
                                        start=False, stop=(source is gath[s] and j == TILES - 1 and k == PARTS - 1))

            def first_layer(n, s):
                c = n * SLOTS + s
                d = s % 2
                pe.wait_ge(onehot_made, c + 1)
                pe.wait_ge(win_in[s], 32 * (n + 1))
                for k in range(PARTS):
                    rows = WIN + PARTS ** 2 if k == 0 else WIN
                    nc.tensor.matmul(z1[d][0:F, :], window[s][0:rows, k, :], onehot[s][0:rows, :], start=(k == 0),
                                     stop=False)
                with pe.If(all_fit == 0):
                    pe.wait_ge(b_in[s], 16 * TILES * (n + 1))
                    for j in range(TILES):
                        for k in range(PARTS):
                            picked(s, gath_b[s], j, k)
                with pe.Else():
                    pass
                if s in DENSE:
                    pe.wait_ge(dense_copied, n * len(DENSE) + DENSE.index(s) + 1)
                else:
                    pe.wait_ge(a_in[s], 16 * TILES * (n + 1))
                for j in range(TILES):
                    for k in range(PARTS):
                        last = picked(s, gath[s], j, k)
                last.then_inc(z1_made, 1)

            for w in range(DENSE_LEAD):
                for part in range(2):
                    dense_products(0, w, part, opening=True)
            pe.wait_ge(weights_in, LOADED_W)
            first_layer(0, 0)
            first_layer(0, 1)

            def sum_by_src(n, s):
                c = n * SLOTS + s
                d = s % 2
                pe.wait_ge(same_made, c + 1)
                pe.wait_ge(message_made, c + 1)
                for j in range(TILES):
                    last = nc.tensor.matmul(zs[d][:, j * (F + 1):(j + 1) * (F + 1)], same[d][:, j, :],
                                            message[d][:, j, :], start=True, stop=True)
                last.then_inc(sum_made, 1)

            def step(n, s, before, after):
                c = n * SLOTS + s
                d = s % 2
                pe.wait_ge(e1_made, c + 1)
                for j in range(TILES):
                    last = nc.tensor.matmul(z2[d][:, j * F:(j + 1) * F], e1[d][:, j * P:(j + 1) * P], we2[:, :],
                                            start=True, stop=True)
                last.then_inc(z2_made, 1)
                if before:
                    sum_by_src(*previous(n, s))
                if after >= DENSE_LEAD:
                    dense_products(*ahead(n, s, DENSE_LEAD), 0)
                if after >= 2:
                    first_layer(*ahead(n, s, 2))
                if after >= DENSE_LEAD:
                    dense_products(*ahead(n, s, DENSE_LEAD), 1)

            chunk_rounds(pe, step)
            sum_by_src(ROUNDS - 1, SLOTS - 1)

            def agg_transposed(g):
                pe.wait_ge(agg_made, g + 1)
                for i, q in enumerate(NODE_PAIRS[g]):
                    last = nc.tensor.matmul(Y_BANKS[g][:, i * NP:(i + 1) * NP],
                                            aggs[0][:, 2 * q:2 * q + 2, :].rearrange("p b f -> p (b f)"),
                                            ident[0:NP, 0:NP], start=True, stop=True)
                last.then_inc(aggT_in_psum, 1)

            def second_product(g):
                pe.wait_ge(n1_made, g + 1)
                for i, q in enumerate(NODE_PAIRS[g]):
                    last = nc.tensor.matmul(Y_BANKS[g][0:NP, i * 2 * F:(i + 1) * 2 * F], n1[:, q * NP:(q + 1) * NP],
                                            wn2[:, :], start=True, stop=True)
                last.then_inc(y_made, 1)

            pe.wait_ge(sum_copied, CHUNKS)
            pe.wait_ge(scattered[ACCS - 1], after_scatters(CHUNKS))
            for g, own in enumerate(NODE_PAIRS):
                o, w = own[0] * NP, len(own) * NP
                nc.tensor.matmul(NODE_BANKS[g][:, 0:w], wn1[:, 0, :], hT[:, o:o + w], start=True, stop=False)
            agg_transposed(0)
            for g, own in enumerate(NODE_PAIRS):
                o, w = own[0] * NP, len(own) * NP
                if g + 1 < len(NODE_PAIRS):
                    agg_transposed(g + 1)
                pe.wait_ge(aggT_taken, g + 1)
                nc.tensor.matmul(NODE_BANKS[g][:, 0:w], wn1[:, 1, :], aggT[:, o:o + w], start=False,
                                 stop=True).then_inc(z3_made, 1)
                if g:
                    second_product(g - 1)
            second_product(len(NODE_PAIRS) - 1)


_INS = ['x', 'src', 'dst', 'edge_attr_3', 'L0_gnn_We1', 'L0_gnn_be1', 'L0_gnn_We2', 'L0_gnn_be2', 'L0_gnn_Wa',
        'L0_gnn_ba', 'L0_gnn_Wn1', 'L0_gnn_bn1', 'L0_gnn_Wn2', 'L0_gnn_bn2']


def kernel(**inputs):
    import numpy as _np
    import concourse.bacc as _bacc
    from concourse import mybir as _mybir
    from concourse.bass_utils import run_bass_kernel_spmd as _run

    nc = _bacc.Bacc("TRN2", target_bir_lowering=False, num_devices=1)
    arrays, args = {}, []
    for name in _INS:
        a = _np.ascontiguousarray(inputs[name])
        arrays[f"in_{name}_dram"] = a
        args.append(nc.dram_tensor(f"in_{name}_dram", a.shape, _mybir.dt.from_np(a.dtype), kind="ExternalInput").ap())
    args.append(nc.dram_tensor("out_dram", inputs['x'].shape, _mybir.dt.float32, kind="ExternalOutput").ap())
    graph_layer(nc, *args)
    r = _run(nc, [arrays], core_ids=[0])
    return r.results[0]["out_dram"]
```
